# Optimizing a Trainium2 kernel written in Bass

```python
import numpy as np
import jax
import jax.numpy as jnp

def _softmax(x, axis=-1):
    return jax.nn.softmax(x, axis=axis)

def _gelu(x):
    return jax.nn.gelu(x, approximate=True)

def _silu(x):
    return jax.nn.silu(x)

def _sigmoid(x):
    return jax.nn.sigmoid(x)

def _layernorm(x, axis=-1, eps=1e-05):
    m = jnp.mean(x, axis=axis, keepdims=True)
    v = jnp.var(x, axis=axis, keepdims=True)
    return (x - m) / jnp.sqrt(v + eps)

def _scatter_add(tgt, idx, src, axis=0):
    return tgt.at[idx].add(src)

def _segment_sum(src, seg, n):
    return jax.ops.segment_sum(src, seg, n)
kernel_name = 'mk_adaln_d1_jaxref_r4_bd4b18'

def setup_inputs(seed: int=0):
    np.random.seed(seed)
    _w = jnp.asarray

    def _L0_attn_setup():
        import jax, jax.numpy as jnp
        import numpy as np
        LN_EPS = 1e-05
        key = jax.random.key(seed)
        ks = jax.random.split(key, 4)
        B_, S, D = (32, 256, 256)
        return {'x': jax.random.normal(ks[0], (B_, S, D), dtype=jnp.float32), 'A': jax.random.normal(ks[1], (D, D), dtype=jnp.float32) * 0.01, 'B': jax.random.normal(ks[2], (D, D), dtype=jnp.float32) * 0.01, 'C': jax.random.normal(ks[3], (D, D), dtype=jnp.float32) * 0.01, 'gamma': jnp.ones((D,), dtype=jnp.float32), 'beta': jnp.zeros((D,), dtype=jnp.float32)}
    _L0_attn_in = _L0_attn_setup()

    def _L0_ffn_setup():
        import jax, jax.numpy as jnp
        import numpy as np
        from jax import lax
        T, B, I, M, O = (64, 64, 256, 256, 256)

        def _xavier(key, shape):
            fan_out, fan_in = shape
            limit = float(np.sqrt(6.0 / (fan_in + fan_out)))
            return jax.random.uniform(key, shape, jnp.float32, -limit, limit)
        key = jax.random.key(seed)
        ks = jax.random.split(key, 9)
        x = jax.random.normal(ks[0], (T, B, I), jnp.float32)
        return {'x': x, 'wf': _xavier(ks[1], (M, I)), 'uf': _xavier(ks[2], (M, M)), 'bf': jnp.zeros((M,), jnp.float32), 'wi': _xavier(ks[3], (M, I)), 'ui': _xavier(ks[4], (M, M)), 'bi': jnp.zeros((M,), jnp.float32), 'wc': _xavier(ks[5], (M, I)), 'uc': _xavier(ks[6], (M, M)), 'bc': jnp.zeros((M,), jnp.float32), 'wo': _xavier(ks[7], (O, I)), 'uo': _xavier(ks[8], (O, M)), 'bo': jnp.zeros((O,), jnp.float32), 'in_c': jnp.zeros((M,), jnp.float32)}
    _L0_ffn_in = _L0_ffn_setup()
    _L0_c = _w((lambda *s: np.random.randn(*s).astype(np.float32) * 0.05)(8, 256))
    _L0_wmod = _w((lambda *s: np.random.randn(*s).astype(np.float32) * 0.05)(256, 6 * 256) * 256 ** (-0.5))
    _d = {'L0_attn_x': _L0_attn_in['x'], 'L0_attn_A': _L0_attn_in['A'], 'L0_attn_B': _L0_attn_in['B'], 'L0_attn_C': _L0_attn_in['C'], 'L0_attn_gamma': _L0_attn_in['gamma'], 'L0_attn_beta': _L0_attn_in['beta'], 'L0_ffn_wf': _L0_ffn_in['wf'], 'L0_ffn_uf': _L0_ffn_in['uf'], 'L0_ffn_bf': _L0_ffn_in['bf'], 'L0_ffn_wi': _L0_ffn_in['wi'], 'L0_ffn_ui': _L0_ffn_in['ui'], 'L0_ffn_bi': _L0_ffn_in['bi'], 'L0_ffn_wc': _L0_ffn_in['wc'], 'L0_ffn_uc': _L0_ffn_in['uc'], 'L0_ffn_bc': _L0_ffn_in['bc'], 'L0_ffn_wo': _L0_ffn_in['wo'], 'L0_ffn_uo': _L0_ffn_in['uo'], 'L0_ffn_bo': _L0_ffn_in['bo'], 'L0_ffn_in_c': _L0_ffn_in['in_c'], 'L0_c': _L0_c, 'L0_wmod': _L0_wmod}
    _x0 = _d['L0_attn_x']
    _d['L0_attn_x'] = jax.random.normal(jax.random.fold_in(jax.random.key(seed), 1), (8, 1024, 256), dtype=_x0.dtype)
    del _x0
    return _d

def reference(L0_attn_x, L0_attn_A, L0_attn_B, L0_attn_C, L0_attn_gamma, L0_attn_beta, L0_ffn_wf, L0_ffn_uf, L0_ffn_bf, L0_ffn_wi, L0_ffn_ui, L0_ffn_bi, L0_ffn_wc, L0_ffn_uc, L0_ffn_bc, L0_ffn_wo, L0_ffn_uo, L0_ffn_bo, L0_ffn_in_c, L0_c, L0_wmod):

    def _L0_attn_ref(x, A, B, C, gamma, beta):
        import jax, jax.numpy as jnp
        import numpy as np
        LN_EPS = 1e-05
        batch, seq_len, d = x.shape
        xb = jnp.einsum('bsd,ed->sbe', x, B)

        def step(h, xb_t):
            h = jnp.tanh(h @ A.T + xb_t)
            y = h @ C.T
            return (h, y)
        h0 = jnp.zeros((batch, d), dtype=x.dtype)
        _, ys = jax.lax.scan(step, h0, xb)
        out = jnp.transpose(ys, (1, 0, 2)) + x
        mu = jnp.mean(out, axis=-1, keepdims=True)
        var = jnp.mean(jnp.square(out - mu), axis=-1, keepdims=True)
        return (out - mu) * jax.lax.rsqrt(var + LN_EPS) * gamma + beta

    def _L0_ffn_ref(x, wf, uf, bf, wi, ui, bi, wc, uc, bc, wo, uo, bo, in_c):
        import jax, jax.numpy as jnp
        import numpy as np
        from jax import lax
        T, B, I, M, O = (64, 64, 256, 256, 256)

        def _xavier(key, shape):
            fan_out, fan_in = shape
            limit = float(np.sqrt(6.0 / (fan_in + fan_out)))
            return jax.random.uniform(key, shape, jnp.float32, -limit, limit)
        batch = x.shape[1]
        c0 = jnp.broadcast_to(in_c, (batch, in_c.shape[0]))

        def step(c, xt):
            ft = jax.nn.sigmoid(xt @ wf.T + c @ uf.T + bf)
            it = jax.nn.sigmoid(xt @ wi.T + c @ ui.T + bi)
            gt = jnp.tanh(xt @ wc.T + c @ uc.T + bc)
            c = ft * c + it * gt
            return (c, None)
        c_final, _ = lax.scan(step, c0, x)
        h = jnp.tanh(jnp.einsum('tbi,oi->tbo', x, wo) + c_final @ uo.T + bo)
        return h
    x = L0_attn_x
    mod = (_silu(L0_c) @ L0_wmod).reshape(L0_c.shape[0], 6, 1, -1)
    sa, ca, ga, sb, cb, gb = (mod[:, 0], mod[:, 1], mod[:, 2], mod[:, 3], mod[:, 4], mod[:, 5])
    ga = (2 * (ga >= 0) - 1) * jnp.maximum(jnp.abs(ga), 0.25)
    gb = (2 * (gb >= 0) - 1) * jnp.maximum(jnp.abs(gb), 0.25)
    h = _layernorm(x, axis=-1) * (1 + ca) + sa
    x = x + ga * _L0_attn_ref(h, L0_attn_A, L0_attn_B, L0_attn_C, L0_attn_gamma, L0_attn_beta)
    h = _layernorm(x, axis=-1) * (1 + cb) + sb
    x = x + gb * _L0_ffn_ref(h, L0_ffn_wf, L0_ffn_uf, L0_ffn_bf, L0_ffn_wi, L0_ffn_ui, L0_ffn_bi, L0_ffn_wc, L0_ffn_uc, L0_ffn_bc, L0_ffn_wo, L0_ffn_uo, L0_ffn_bo, L0_ffn_in_c)
    return x

_drawn_inputs = setup_inputs


def setup_inputs(seed=0):
    import zlib

    import numpy as np

    out = dict(_drawn_inputs(seed))
    spreads = {'L0_attn_gamma': (1.0, 0.2),
     'L0_attn_beta': (0.0, 0.36),
     'L0_ffn_bf': (0.0, 0.8),
     'L0_ffn_bi': (0.0, 0.8),
     'L0_ffn_bc': (0.0, 0.657),
     'L0_ffn_bo': (0.0, 0.489),
     'L0_ffn_in_c': (0.0, 0.8)}
    factors = {'L0_attn_A': 8.0,
     'L0_attn_B': 8.0,
     'L0_attn_C': 8.0,
     'L0_ffn_wf': 2.867,
     'L0_ffn_uf': 5.144,
     'L0_ffn_ui': 4.082}
    for name, (base, spread) in spreads.items():
        noise = np.random.default_rng([zlib.crc32(name.encode()), seed]).standard_normal(out[name].shape)
        drawn = base * np.exp(spread * noise) if base else spread * noise
        out[name] = jnp.asarray(drawn.astype(out[name].dtype))
    for name, factor in factors.items():
        out[name] = (out[name] * factor).astype(out[name].dtype)
    return out
```

```python
import concourse.bass as bass
from concourse import mybir
from contextlib import ExitStack



class At:

    def __init__(self, i, c):
        self.i, self.c = i, c

    def lin(self, k, c0=0):
        c = k * self.c + c0
        return c if isinstance(self.i, int) else self.i * (2 * k) + c

    def half(self, k, back, c0=0):
        c = k * ((self.c - back) // 2) + c0
        return c if isinstance(self.i, int) else self.i * k + c


def adaln_kernel(nc, x, A, B, C, gamma, beta, wf, uf, bf, wi, ui, bi, wc, uc, bc, wo, uo, bo, in_c, cond, wmod, out):
    f32 = mybir.dt.float32
    f32r = mybir.dt.float32r
    i32 = mybir.dt.int32
    ALU = mybir.AluOpType
    ACT = mybir.ActivationFunctionType
    AX = mybir.AxisListType

    P = 128
    NB, S, D = x.shape
    K = P // NB
    L = S // K
    H = D // P
    SKIP = 8
    PAIRS = L // 2
    SP0 = SKIP // 2
    RP1 = PAIRS - SP0
    W = 2 * D
    GROUP = 8
    NG = PAIRS // GROUP
    GC = 2 * GROUP * K
    RING = 2 * GROUP
    EPS = 1e-5
    TOL = 2.0 ** -18

    G0 = GROUP + 2
    O0 = 2 * GROUP + 2
    UNITS2 = O0 + PAIRS + 1
    R1LAG = 4
    UNITS1 = PAIRS + 3

    x_v = x.rearrange("b (k t) d -> (b k) (t d)", k=K)
    out_v = out.rearrange("b (k t) d -> (b k) (t d)", k=K)
    h_park = nc.dram_tensor("h_park", [PAIRS, P, W], f32, kind="Internal").ap()

    ctx = ExitStack()
    with ctx:
        def sb(name, shape, dt=f32):
            return ctx.enter_context(nc.sbuf_tensor(name, shape, dt))

        def sem(name):
            return ctx.enter_context(nc.semaphore(name))

        ident = sb("ident", [P, P])
        ones = sb("ones", [P, 1])
        mhalf = sb("mhalf", [P, 2])
        epst = sb("epst", [P, 2])
        AT = sb("AT", [P, H, D])
        BT = sb("BT", [P, H, D])
        CT = sb("CT", [P, H, D])
        uoT = sb("uoT", [P, H, D])
        SPLIT = ["wf", "wi", "wc", "uf", "ui", "uc", "wo"]
        whi = {n: sb(n + "T_hi", [P, H, D], f32r) for n in SPLIT}
        wlo = {n: sb(n + "T_lo", [P, H, D], f32r) for n in SPLIT}
        ca1 = sb("ca1", [P, D])
        sa = sb("sa", [P, D])
        gag = sb("gag", [P, D])
        gab = sb("gab", [P, D])
        cb1 = sb("cb1", [P, D])
        sbt = sb("sbt", [P, D])
        gbT = sb("gbT", [P, H, NB])
        bias = sb("bias", [P, 4, H])
        c0 = sb("c0", [P, H])
        c0hi = sb("c0hi", [P, H], f32r)
        c0lo = sb("c0lo", [P, H], f32r)

        state = sb("state", [P, PAIRS * W])
        hi = sb("hi", [P, 2, H, NB, GC], f32r)
        lo = sb("lo", [P, 2, H, NB, GC], f32r)
        xin = sb("xin", [P, 2, W])
        htok = sb("htok", [P, 2, W])
        h2tok = sb("h2tok", [P, W])
        hT = sb("hT", [P, 2, W])
        y = hT[:, 0, :]
        ow = hT[:, 1, :]
        outb = sb("outb", [P, W])
        pre = sb("pre", [P, D])
        hs = sb("hs", [P, 2, H, P])
        h_skip = sb("h_skip", [P, D])
        h_end = sb("h_end", [P, D])
        gf = sb("gf", [P, H, GC])
        gi = sb("gi", [P, H, GC])
        gg = sb("gg", [P, H, GC])
        cst = sb("cst", [P, H, GC])
        chi = sb("chi", [P, H, GC], f32r)
        clo = sb("clo", [P, H, GC], f32r)
        uvec = sb("uvec", [P, H, GC])
        st = sb("st", [P, 2, 6])
        mv = sb("mv", [P, 2, 2])
        mvb = sb("mvb", [P, 2, 2])
        ve = sb("ve", [P, 2])
        rstd = sb("rstd", [P, 2])
        rstdb = sb("rstdb", [P, 2])
        cnt = sb("cnt", [P, 1])
        miss = sb("miss", [1, 1])
        again = sb("again", [1, 1], i32)

        NAMES = ["A", "B", "C", "wf", "wi", "wc", "uf", "ui", "uc", "wo", "uo"]
        raw = {n: state[:, i * W:(i + 1) * W].rearrange("p (m d) -> p m d", m=H) for i, n in enumerate(NAMES)}
        at = len(NAMES) * W
        wm = state[:, at:at + 6 * W].rearrange("p (k n) -> p k n", k=H)
        at += 6 * W
        gamma_b = state[:, at:at + D]
        beta_b = state[:, at + D:at + 2 * D]
        cn = state[0:NB, at + W:at + W + D]
        csig = state[0:NB, at + W + D:at + 2 * W]
        at += 2 * W
        scT = state[:, at:at + H * NB].rearrange("p (k b) -> p k b", k=H)
        at += H * NB
        scE = state[:, at:at + H * P].rearrange("p (k b n) -> p k b n", k=H, b=NB)
        at += H * P
        ga = state[:, at:at + D]
        gmag = state[:, at + D:at + 2 * D]
        gs = state[:, at + 2 * D:at + 2 * D + H * NB].rearrange("p (k b) -> p k b", k=H)
        gm = state[:, at + 3 * D:at + 3 * D + H * NB].rearrange("p (k b) -> p k b", k=H)

        def bank(name):
            return ctx.enter_context(nc.psum_tensor(name, [P, 512], f32))

        psR, psC, psT, psF, psI, psG, psW, psO = (bank(n) for n in (
            "psR", "psC", "psT", "psF", "psI", "psG", "psW", "psO"))
        psB = psW

        q_ident = sem("q_ident")
        q_w = {n: sem("q_w_" + n) for n in NAMES}
        q_cond = sem("q_cond")
        q_small = sem("q_small")
        q_act = sem("q_act")
        q_dve = sem("q_dve")
        q_pe = sem("q_pe")
        q_silu = sem("q_silu")
        q_scT = sem("q_scT")
        q_scTp = sem("q_scTp")
        q_mod = sem("q_mod")
        q_gb = sem("q_gb")
        q_sig = sem("q_sig")
        q_ready = sem("q_ready")
        q_actready = sem("q_actready")

        a_x = [sem(f"a_xin{i}") for i in range(2)]
        a_stats = sem("a_stats")
        a_mv = sem("a_mv")
        a_ve = sem("a_ve")
        a_rstd = sem("a_rstd")
        a_tmp = sem("a_tmp")
        a_h = sem("a_h")
        a_park = [sem(f"a_park{i}") for i in range(2)]
        a_T = sem("a_T")
        a_hT = sem("a_hT")
        a_B = sem("a_B")
        a_xb = sem("a_xb")
        a_r = sem("a_r")
        a_pre = sem("a_pre")
        a_tanh = sem("a_tanh")
        a_end = sem("a_end")
        s_x = [sem(f"s_xin{i}") for i in range(2)]
        s_h = [sem(f"s_hin{i}") for i in range(2)]
        s_r = sem("s_r")
        s_pre = sem("s_pre")
        s_tanh = sem("s_tanh")
        s_skip = sem("s_skip")
        s_C = sem("s_C")
        s_y = sem("s_y")
        s_stA = sem("s_stA")
        s_mvA = sem("s_mvA")
        s_veA = sem("s_veA")
        s_rA = sem("s_rA")
        s_tmpA = sem("s_tmpA")
        s_xg = sem("s_xg")
        s_x1 = sem("s_x1")
        s_stB = sem("s_stB")
        s_mvB = sem("s_mvB")
        s_veB = sem("s_veB")
        s_rB = sem("s_rB")
        s_tmpB = sem("s_tmpB")
        s_h2 = sem("s_h2")
        s_T = sem("s_T")
        s_hi = sem("s_hi")
        s_lo = sem("s_lo")
        s_gate = sem("s_gate")
        s_f = sem("s_f")
        s_i = sem("s_i")
        s_g = sem("s_g")
        s_fc = sem("s_fc")
        s_ig = sem("s_ig")
        s_c = sem("s_c")
        s_chi = sem("s_chi")
        s_clo = sem("s_clo")
        s_U = sem("s_U")
        s_u = sem("s_u")
        s_W = sem("s_W")
        s_ws = sem("s_ws")
        s_ot = sem("s_ot")
        s_ob = sem("s_ob")
        s_TO = sem("s_TO")
        s_fin = sem("s_fin")
        s_out = sem("s_out")
        k_diff = sem("k_diff")
        k_sum = sem("k_sum")
        k_flag = sem("k_flag")
        s_apart = sem("s_apart")
        per_round = [*a_x, a_stats, a_mv, a_ve, a_rstd, a_tmp, a_h, *a_park, a_T, a_hT, a_B, a_xb, a_r, a_pre,
                     a_tanh, a_end, *s_x, *s_h, s_r, s_pre, s_tanh, s_skip, s_C, s_y, s_stA, s_mvA, s_veA, s_rA,
                     s_tmpA, s_xg, s_x1, s_stB, s_mvB, s_veB, s_rB, s_tmpB, s_h2, s_T, s_hi, s_lo, s_gate, s_f,
                     s_i, s_g, s_fc, s_ig, s_c, s_chi, s_clo, s_U, s_u, s_W, s_ws, s_ot, s_ob, s_TO, s_fin,
                     s_out, k_diff, k_sum, k_flag, s_apart]
        r_over = sem("r_over")
        r_next = sem("r_next")

        def ranges(cuts, end):
            return list(zip(cuts, cuts[1:] + [end]))

        RUNS1 = ranges([0, 1, 2, 3, 4, 5, RP1, RP1 + 1, RP1 + 2, RP1 + 3, RP1 + 4, RP1 + 5, RP1 + 6], UNITS1)
        cuts = {0, 1, 2, 3, 4, PAIRS, PAIRS + 1, O0 + 1, O0 + 2, UNITS2 - 1}
        for g in range(NG + 1):
            cuts |= {G0 + GROUP * g, G0 + GROUP * g + 1, G0 + GROUP * g - 1}
        RUNS2 = ranges(sorted(c for c in cuts if c < UNITS2 and c != G0 - 1), UNITS2)

        def walk(eng, runs, unit):
            for a, b in runs:
                n = (b - a) // 2
                if n < 2:
                    n = 0
                if n:
                    with eng.Fori(0, n) as i:
                        unit(At(i, a), a)
                        unit(At(i, a + 1), a + 1)
                for c in range(a + 2 * n, b):
                    unit(At(0, c), c)

        def pair1(v, ref, back):
            return v.lin(1, SP0 - back) if ref - back < RP1 else v.lin(1, -RP1 - back)

        def has(ref, first, n):
            return first <= ref < first + n

        def grp(ref):
            return (ref - G0) // GROUP

        def pos(ref):
            return (ref - G0) % GROUP

        def row(v, k, off=0, n=W):
            return state[:, bass.ds(v * W + off, n)] if not isinstance(v, int) else state[:, v * W + off:v * W + off + n]

        def tposed(m):
            return psT[:, m * 2 * P:(m + 1) * 2 * P].rearrange("p (t b k) -> p t b k", t=2, b=NB)

        def ring(buf, v, ref, back, m):
            g, p = (ref - back) // GROUP, v.lin(1, -back - GROUP * ((ref - back) // GROUP))
            part = buf[:, g % 2, m, :, bass.ds(p * (2 * K), 2 * K)]
            return part.rearrange("p b (t k) -> p t b k", t=2)

        def apart(eng):
            eng.sem_inc(s_apart, 1)

        def rounds(eng, body, name):
            left = eng.alloc_register("rounds_" + name)
            eng.reg_mov(left, K)
            with eng.Fori(0, left) as r:
                body()
                eng.wait_ge(k_flag, 1)
                eng.reg_mov(left, eng.value_load(again[0:1, 0:1], min_val=0, max_val=K))
                eng.drain().then_inc(r_over, 1)
                eng.wait_ge(r_next, r + 1)

        block = ctx.enter_context(nc.Block())

        @block.sync
        def _(sp):
            for n, w in zip(NAMES, (A, B, C, wf, wi, wc, uf, ui, uc, wo, uo)):
                if n == "A":
                    sp.dma_start(cn, cond).then_inc(q_cond, 16)
                    sp.dma_start(wm, wmod.rearrange("(k p) n -> p k n", p=P)).then_inc(q_small, 16)
                    for dst, src in ((gamma_b, gamma), (beta_b, beta)):
                        sp.dma_start(dst, src.rearrange("(o n) -> o n", o=1).broadcast_to([P, D])).then_inc(q_small, 16)
                    for j, src in enumerate((bf, bi, bc, bo)):
                        sp.dma_start(bias[:, j, :], src.rearrange("(m p) -> p m", p=P), allow_slow_non_contiguous=True).then_inc(q_small, 16)
                    sp.dma_start(c0[:, :], in_c.rearrange("(m p) -> p m", p=P), allow_slow_non_contiguous=True).then_inc(q_small, 16)
                sp.dma_start(raw[n], w.rearrange("(m p) d -> p m d", p=P)).then_inc(q_w[n], 16)

            def unit1(v, ref):
                if has(ref, 0, PAIRS):
                    if ref >= 2:
                        sp.wait_ge(a_h, v.lin(2, -2))
                    p = pair1(v, ref, 0)
                    sp.dma_start(xin[:, ref % 2, :], x_v[:, bass.ds(p * W, W)]).then_inc(a_x[ref % 2], 16)
                if has(ref, 2, PAIRS):
                    sp.wait_ge(a_h, v.lin(2, -2))
                    p = pair1(v, ref, 2)
                    sp.dma_start(h_park[bass.ds(p, 1), :, :].rearrange("o p w -> p (o w)"),
                                 htok[:, ref % 2, :]).then_inc(a_park[ref % 2], 16)

            def unit2(v, ref):
                if has(ref, 0, PAIRS):
                    if ref >= 2:
                        sp.wait_ge(s_x1, v.lin(2, -2))
                    sp.dma_start(xin[:, ref % 2, :], x_v[:, bass.ds(v.lin(W), W)]).then_inc(s_x[ref % 2], 16)
                    sp.dma_start(htok[:, ref % 2, :],
                                 h_park[bass.ds(v.lin(1), 1), :, :].rearrange("o p w -> p (o w)")).then_inc(s_h[ref % 2], 16)
                if has(ref, O0 + 1, PAIRS):
                    sp.wait_ge(s_fin, v.lin(1, -O0))
                    sp.dma_start(out_v[:, bass.ds(v.lin(W, -(O0 + 1) * W), W)], outb[:, :]).then_inc(s_out, 16)

            left = sp.alloc_register("rounds_sp")
            sp.reg_mov(left, K)
            with sp.Fori(0, left) as r:
                walk(sp, RUNS1, unit1)
                sp.wait_ge(a_park[0], 16 * (PAIRS // 2))
                sp.wait_ge(a_park[1], 16 * (PAIRS // 2))
                sp.wait_ge(a_T, PAIRS)
                walk(sp, RUNS2, unit2)
                sp.wait_ge(s_out, 16 * PAIRS)
                sp.wait_ge(k_flag, 1)
                sp.reg_mov(left, sp.value_load(again[0:1, 0:1], min_val=0, max_val=K))
                sp.wait_ge(r_over, r * 4 + 4)
                apart(sp)
                for s in per_round:
                    sp.sem_clear(s)
                sp.sem_inc(r_next, 1)

        @block.gpsimd
        def _(pool):
            pool.memset(ident[:, :], 0.0).then_inc(q_ident, 1)
            pool.wait_ge(q_ident, 1)
            pool.affine_select(out=ident[:, :], in_=ident[:, :], compare_op=ALU.not_equal, fill=1.0, base=0,
                               pattern=[[-1, P]], channel_multiplier=1).then_inc(q_ident, 1)
            pool.memset(mhalf[:, :], -0.5).then_inc(q_ident, 1)
            pool.memset(ones[:, :], 1.0).then_inc(q_ident, 1)
            pool.memset(epst[:, :], EPS).then_inc(q_ident, 1)
            pool.memset(h_skip[:, :], 0.0).then_inc(q_ident, 1)
            pool.wait_ge(q_ident, 6)
            pool.wait_ge(q_ready, 1)

            def unit1(v, ref):
                if has(ref, 0, PAIRS):
                    pool.wait_ge(a_mv, v.lin(2, 2))
                    pool.tensor_tensor(ve[:, :], mv[:, :, 1], epst[:, :], ALU.add).then_inc(a_ve, 1)
                    pool.wait_ge(a_ve, v.lin(1, 1))
                    pool.tensor_tensor(rstd[:, :], ve[:, :], mhalf[:, :], ALU.pow).then_inc(a_rstd, 1)

            def unit2(v, ref):
                if has(ref, G0 + 1, PAIRS):
                    pool.wait_ge(s_i, v.lin(2, -2 * G0))
                    pool.wait_ge(s_g, v.lin(2, -2 * G0))
                    pool.tensor_tensor(gi[:, :, :], gi[:, :, :], gg[:, :, :], ALU.mult).then_inc(s_ig, 1)
                if has(ref, 1, PAIRS):
                    pool.wait_ge(s_x[(ref - 1) % 2], v.half(16, 1, 16))
                    xg = xin[:, (ref - 1) % 2, :].rearrange("p (t d) -> p t d", t=2)
                    pool.tensor_tensor(xg, xg, gab[:, :].rearrange("p (o d) -> p o d", o=1).broadcast_to([P, 2, D]),
                                       ALU.add).then_inc(s_xg, 1)
                    pool.wait_ge(s_mvA, v.lin(2))
                    pool.tensor_tensor(ve[:, :], mv[:, :, 1], epst[:, :], ALU.add).then_inc(s_veA, 1)
                    pool.wait_ge(s_veA, v.lin(1))
                    pool.tensor_tensor(rstd[:, :], ve[:, :], mhalf[:, :], ALU.pow).then_inc(s_rA, 1)
                    pool.wait_ge(s_mvB, v.lin(2))
                    pool.wait_ge(s_rA, v.lin(1))
                    pool.tensor_tensor(ve[:, :], mvb[:, :, 1], epst[:, :], ALU.add).then_inc(s_veB, 1)
                    pool.wait_ge(s_veB, v.lin(1))
                    pool.tensor_tensor(rstdb[:, :], ve[:, :], mhalf[:, :], ALU.pow).then_inc(s_rB, 1)
                if has(ref, O0, PAIRS):
                    pool.wait_ge(s_ot, v.lin(1, -O0 + 1))
                    for m in range(H):
                        o4 = ow[:, m * GC:(m + 1) * GC].rearrange("p (t b k) -> p t b k", t=2, b=NB)
                        g4 = gbT[:, m:m + 1, :].rearrange("p o (b k) -> p o b k", k=1).broadcast_to([P, 2, NB, K])
                        pool.tensor_tensor(o4, o4, g4, ALU.mult).then_inc(s_ob, 1)

            def body():
                walk(pool, RUNS1, unit1)
                walk(pool, RUNS2, unit2)

            rounds(pool, body, "pool")

        @block.scalar
        def _(act):
            act.wait_ge(q_cond, 16)
            act.activation(csig, cn, ACT.Sigmoid).then_inc(q_sig, 1)
            for n, name in enumerate(NAMES):
                act.wait_ge(q_pe, n + 1)
                dst = {"A": AT, "B": BT, "C": CT, "uo": uoT}.get(name)
                dst = whi[name] if dst is None else dst
                src = (psF, psI, psG)[n % 3]
                act.activation(dst[:, :, :], src[:, :].rearrange("p (k d) -> p k d", k=H), ACT.Copy).then_inc(q_act, 1)
            act.wait_ge(q_ready, 1)

            def tanhs(sem_in, sem_out, v, tt, back, apart):
                if not apart:
                    act.wait_ge(sem_in, v.lin(4, -4 * back + 2 * tt + H))
                    act.activation(hs[:, tt, :, :], pre[:, :].rearrange("p (m n) -> p m n", m=H), ACT.Tanh).then_inc(sem_out, H)
                    return
                for m in range(H):
                    act.wait_ge(sem_in, v.lin(4, -4 * back + 2 * tt + m + 1))
                    act.activation(hs[:, tt, m, :], pre[:, m * P:(m + 1) * P], ACT.Tanh).then_inc(sem_out, 1)

            def unit1(v, ref):
                rec = has(ref, R1LAG, RP1)
                if rec:
                    tanhs(a_pre, a_tanh, v, 0, R1LAG, True)
                if has(ref, 2, PAIRS):
                    act.wait_ge(a_T, v.lin(1, -1))
                    if ref >= 4:
                        act.wait_ge(a_B, v.lin(1, -3))
                    act.activation(hT[:, ref % 2, :], psT[:, :], ACT.Copy).then_inc(a_hT, 1)
                if rec:
                    tanhs(a_pre, a_tanh, v, 1, R1LAG, True)
                if has(ref, 3, PAIRS):
                    act.wait_ge(a_B, v.lin(1, -2))
                    act.activation(row(pair1(v, ref, 3), 1), psB[:, :], ACT.Copy).then_inc(a_xb, 1)

            def unit2(v, ref):
                if has(ref, 0, PAIRS):
                    tanhs(s_pre, s_tanh, v, 0, 0, ref < G0)
                if has(ref, G0 + 1, PAIRS) and pos(ref - 1) < GROUP - 1:
                    act.wait_ge(s_c, v.lin(1, -G0))
                    act.activation(chi[:, :, :], cst[:, :, :], ACT.Copy).then_inc(s_chi, 1)
                if has(ref, 2, PAIRS):
                    act.wait_ge(s_T, v.lin(1, -1))
                    for m in range(H):
                        act.activation(ring(hi, v, ref, 2, m), tposed(m), ACT.Copy).then_inc(s_hi, 1)
                if has(ref, O0, PAIRS) and pos(ref) == 0:
                    act.wait_ge(s_U, (ref - O0) // GROUP + 1)
                    if ref > O0:
                        act.wait_ge(s_ws, 2 * (ref - O0))
                    for m in range(H):
                        act.activation(uvec[:, m, :], psC[:, m * GC:(m + 1) * GC], ACT.Identity,
                                       bias=bias[:, 3, m:m + 1]).then_inc(s_u, 1)
                if has(ref, 0, PAIRS):
                    tanhs(s_pre, s_tanh, v, 1, 0, ref < G0)
                if has(ref, O0, PAIRS):
                    act.wait_ge(s_ws, v.lin(2, -2 * O0 + 2))
                    act.activation(ow, ow, ACT.Tanh).then_inc(s_ot, 1)
                if has(ref, G0, PAIRS):
                    if ref > G0:
                        act.wait_ge(s_c, v.lin(1, -G0))
                    for n, (dst, src, fn, s) in enumerate(((gf, psF, ACT.Sigmoid, s_f), (gi, psI, ACT.Sigmoid, s_i),
                                                           (gg, psG, ACT.Tanh, s_g))):
                        act.wait_ge(s_gate, v.lin(3, -3 * G0 + n + 1))
                        for m in range(H):
                            act.activation(dst[:, m, :], src[:, m * GC:(m + 1) * GC], fn,
                                           bias=bias[:, n, m:m + 1]).then_inc(s, 1)

            def body():
                walk(act, RUNS1, unit1)
                walk(act, RUNS2, unit2)

            rounds(act, body, "act")

        @block.vector
        def _(dve):
            dve.wait_ge(q_ident, 6)
            dve.wait_ge(q_sig, 1)
            dve.tensor_tensor(csig, cn, csig, ALU.mult).then_inc(q_silu, 1)
            dve.wait_ge(q_scTp, 1)
            dve.tensor_copy(scT, psR[:, 0:H * NB].rearrange("p (k b) -> p k b", k=H)).then_inc(q_scT, 1)
            dve.tensor_copy(scE, psR[:, 0:H * NB].rearrange("p (k b o) -> p k b o", k=H, o=1)
                            .broadcast_to([P, H, NB, K])).then_inc(q_scT, 1)
            for n, name in enumerate(NAMES):
                if name in whi:
                    dve.wait_ge(q_act, n + 1)
                    src = (psF, psI, psG)[n % 3]
                    dve.tensor_tensor(wlo[name][:, :, :], src[:, :].rearrange("p (k d) -> p k d", k=H),
                                      whi[name][:, :, :].bitcast(f32), ALU.subtract).then_inc(q_dve, 1)
            n = [0]

            def step(ins):
                n[0] += 1
                ins.then_inc(q_gb, 1)

            def done():
                dve.wait_ge(q_gb, n[0])

            dve.wait_ge(q_small, 16 * 8)
            dve.wait_ge(q_mod, 4)
            step(dve.tensor_copy(sa[:, :], psC[:, 0:D]))
            step(dve.tensor_scalar(ca1[:, :], psC[:, D:W], 1.0, None, ALU.add))
            step(dve.tensor_copy(sbt[:, :], psT[:, D:W]))
            step(dve.tensor_scalar(cb1[:, :], psO[:, 0:D], 1.0, None, ALU.add))
            gbp = psW[:, 0:H * NB].rearrange("p (k b) -> p k b", k=H)
            for src, up, down in ((psT[:, 0:D], ga, gmag), (gbp, gs, gm)):
                step(dve.tensor_scalar(up, src, 0.25, None, ALU.max))
                step(dve.tensor_scalar(down, src, -0.25, None, ALU.min))
            done()
            for src, up, down in ((psT[:, 0:D], ga, gmag), (gbp, gs, gm)):
                step(dve.scalar_tensor_tensor(up, src, 0.0, up, ALU.is_ge, ALU.mult))
                step(dve.scalar_tensor_tensor(down, src, 0.0, down, ALU.is_lt, ALU.mult))
            done()
            step(dve.tensor_tensor(ga, ga, gmag, ALU.add))
            step(dve.tensor_tensor(gbT[:, :, :], gs, gm, ALU.add))
            done()
            step(dve.tensor_tensor(gag[:, :], ga, gamma_b, ALU.mult))
            step(dve.tensor_tensor(gab[:, :], ga, beta_b, ALU.mult))
            step(dve.tensor_copy(c0hi[:, :], c0[:, :]))
            done()
            step(dve.tensor_tensor(c0lo[:, :], c0[:, :], c0hi[:, :].bitcast(f32), ALU.subtract))
            done()
            dve.wait_ge(q_act, len(NAMES))
            dve.wait_ge(q_dve, len(SPLIT))
            dve.sem_inc(q_ready, 1)

            def adds(sem_in, sem_out, v, tt, back, p, apart):
                if not apart:
                    dve.wait_ge(sem_in, v.lin(4, -4 * back + 2 * tt + H))
                    xb = row(p, 1).rearrange("p (m t n) -> p m t n", m=H, t=2)[:, :, tt, :]
                    dve.tensor_tensor(pre[:, :].rearrange("p (m n) -> p m n", m=H),
                                      psR[:, 0:D].rearrange("p (m n) -> p m n", m=H), xb, ALU.add).then_inc(sem_out, H)
                    return
                for m in range(H):
                    dve.wait_ge(sem_in, v.lin(4, -4 * back + 2 * tt + m + 1))
                    xb = row(p, 1, m * 2 * P + tt * P, P)
                    dve.tensor_tensor(pre[:, m * P:(m + 1) * P], (psR, psF)[m][:, 0:P], xb, ALU.add).then_inc(sem_out, 1)

            def halfw(t, tt):
                return t[:, tt * D:(tt + 1) * D]

            def stats(src, s_in, s_out, v, back, dst):
                for tt in range(2):
                    dve.bn_stats(st[:, tt, :], halfw(src, tt)).then_inc(s_in, 1)
                dve.wait_ge(s_in, v.lin(2, -2 * back + 2))
                apart(dve)
                for tt in range(2):
                    dve.bn_aggr(dst[:, tt, :], st[:, tt, :]).then_inc(s_out, 1)

            def unit1(v, ref):
                rec, norm = has(ref, R1LAG, RP1), has(ref, 1, PAIRS)

                def normalise(tt):
                    if not norm:
                        return
                    src, dst = xin[:, (ref - 1) % 2, :], htok[:, (ref - 1) % 2, :]
                    if tt == 0 and ref >= 3:
                        dve.wait_ge(a_T, v.lin(1, -2))
                        dve.wait_ge(a_park[(ref - 1) % 2], v.half(16, 1))
                    if tt == 0:
                        dve.wait_ge(a_mv, v.lin(2))
                    dve.scalar_tensor_tensor(halfw(dst, tt), halfw(src, tt), mv[:, tt, 0:1], ca1[:, :],
                                             ALU.subtract, ALU.mult).then_inc(a_tmp, 1)
                    dve.wait_ge(a_tmp, v.lin(2, tt - 1))
                    if tt == 0:
                        dve.wait_ge(a_rstd, v.lin(1))
                    dve.scalar_tensor_tensor(halfw(dst, tt), halfw(dst, tt), rstd[:, tt:tt + 1], sa[:, :],
                                             ALU.mult, ALU.add).then_inc(a_h, 1)

                if rec:
                    dve.wait_ge(a_xb, v.lin(1, 1 - R1LAG))
                    adds(a_r, a_pre, v, 0, R1LAG, v.lin(1), True)
                normalise(0)
                if rec:
                    adds(a_r, a_pre, v, 1, R1LAG, v.lin(1), True)
                normalise(1)
                if has(ref, 0, PAIRS):
                    dve.wait_ge(a_x[ref % 2], v.half(16, 0, 16))
                    if norm:
                        dve.wait_ge(a_h, v.lin(2))
                    apart(dve)
                    stats(xin[:, ref % 2, :], a_stats, a_mv, v, 0, mv)

            def unit2(v, ref):
                rec, post, outp = has(ref, 0, PAIRS), has(ref, 1, PAIRS), has(ref, O0, PAIRS)
                bk = (ref - 1) % 2
                if rec:
                    adds(s_r, s_pre, v, 0, 0, v.lin(1), ref < G0)
                if has(ref, G0 + 1, PAIRS):
                    dve.wait_ge(s_fc, v.lin(1, -G0))
                    dve.wait_ge(s_ig, v.lin(1, -G0))
                    dve.tensor_tensor(cst[:, :, :], gf[:, :, :], gi[:, :, :], ALU.add).then_inc(s_c, 1)
                if post:
                    dve.wait_ge(s_C, v.lin(1))
                    dve.wait_ge(s_h[bk], v.half(16, 1, 16))
                    if ref >= 2:
                        dve.wait_ge(s_h2, v.lin(2, -2))
                    dve.tensor_tensor(y, psC[:, :], htok[:, bk, :], ALU.add).then_inc(s_y, 1)
                    dve.wait_ge(s_y, v.lin(1))
                    apart(dve)
                    stats(y, s_stA, s_mvA, v, 1, mv)
                if has(ref, G0 + 1, PAIRS) and pos(ref - 1) < GROUP - 1:
                    dve.wait_ge(s_c, v.lin(1, -G0))
                    dve.wait_ge(s_chi, v.lin(1, -G0 - grp(ref - 1)))
                    dve.tensor_tensor(clo[:, :, :], cst[:, :, :], chi[:, :, :].bitcast(f32), ALU.subtract).then_inc(s_clo, 1)
                if has(ref, 2, PAIRS):
                    for m in range(H):
                        dve.wait_ge(s_hi, v.lin(2, -4 + H))
                        dve.tensor_tensor(ring(lo, v, ref, 2, m), tposed(m), ring(hi, v, ref, 2, m).bitcast(f32),
                                          ALU.subtract).then_inc(s_lo, 1)
                if post:
                    dve.wait_ge(s_mvA, v.lin(2))
                    for tt in range(2):
                        dve.scalar_tensor_tensor(halfw(y, tt), halfw(y, tt), mv[:, tt, 0:1], gag[:, :],
                                                 ALU.subtract, ALU.mult).then_inc(s_tmpA, 1)
                    dve.wait_ge(s_rA, v.lin(1))
                    dve.wait_ge(s_xg, v.lin(1))
                    for tt in range(2):
                        dve.wait_ge(s_tmpA, v.lin(2, -1 + tt))
                        dve.scalar_tensor_tensor(row(v.lin(1, -1), 1, tt * D, D), halfw(y, tt), rstd[:, tt:tt + 1],
                                                 halfw(xin[:, bk, :], tt), ALU.mult, ALU.add).then_inc(s_x1, 1)
                if rec:
                    adds(s_r, s_pre, v, 1, 0, v.lin(1), ref < G0)
                    if ref == SP0 - 1:
                        dve.wait_ge(s_tanh, 4 * SP0)
                        dve.tensor_copy(h_skip[:, :].rearrange("p (m n) -> p m n", m=H), hs[:, 1, :, :]).then_inc(s_skip, 1)
                if post:
                    dve.wait_ge(s_x1, v.lin(2))
                    apart(dve)
                    stats(row(v.lin(1, -1), 1), s_stB, s_mvB, v, 1, mvb)
                if has(ref, O0 + 1, PAIRS):
                    dve.wait_ge(s_TO, v.lin(1, -O0))
                    if ref > O0 + 1:
                        dve.wait_ge(s_out, v.lin(16, -16 * (O0 + 1)))
                    dve.tensor_tensor(outb[:, :], psO[:, :], row(v.lin(1, -O0 - 1), 1), ALU.add).then_inc(s_fin, 1)
                if outp:
                    dve.wait_ge(s_W, v.lin(1, -O0 + 1))
                    if pos(ref) == 0:
                        dve.wait_ge(s_u, 2 * ((ref - O0) // GROUP + 1))
                    if ref > O0:
                        dve.wait_ge(s_TO, v.lin(1, -O0))
                    p = v.lin(1, -O0 - GROUP * ((ref - O0) // GROUP))
                    for m in range(H):
                        dve.tensor_tensor(
                            ow[:, m * GC:(m + 1) * GC].rearrange("p (t b k) -> p b t k", t=2, b=NB),
                            psW[:, m * GC:(m + 1) * GC].rearrange("p (b t k) -> p b t k", b=NB, t=2),
                            uvec[:, m:m + 1, bass.ds(p * (2 * K), 2 * K)].rearrange("p o (t k) -> p o t k", t=2)
                            .broadcast_to([P, NB, 2, K]),
                            ALU.add).then_inc(s_ws, 1)
                if post:
                    dve.wait_ge(s_mvB, v.lin(2))
                    for tt in range(2):
                        dve.scalar_tensor_tensor(halfw(y, tt), row(v.lin(1, -1), 1, tt * D, D), mvb[:, tt, 0:1], cb1[:, :],
                                                 ALU.subtract, ALU.mult).then_inc(s_tmpB, 1)
                    dve.wait_ge(s_rB, v.lin(1))
                    if ref >= 2:
                        dve.wait_ge(s_T, v.lin(1, -1))
                    for tt in range(2):
                        dve.wait_ge(s_tmpB, v.lin(2, -1 + tt))
                        dve.scalar_tensor_tensor(h2tok[:, tt * D:(tt + 1) * D], halfw(y, tt), rstdb[:, tt:tt + 1], sbt[:, :],
                                                 ALU.mult, ALU.add).then_inc(s_h2, 1)
                if has(ref, G0, PAIRS):
                    dve.wait_ge(s_f, v.lin(2, -2 * G0 + 2))
                    if pos(ref) == 0:
                        prev = c0[:, :].rearrange("p (m o) -> p m o", o=1).broadcast_to([P, H, GC])
                    else:
                        prev = cst[:, :, :]
                    dve.tensor_tensor(gf[:, :, :], gf[:, :, :], prev, ALU.mult).then_inc(s_fc, 1)
                if ref == PAIRS + 1:
                    dve.tensor_tensor(pre[:, :].rearrange("p (m n) -> p m n", m=H), hs[:, 1, :, :],
                                      h_end[:, :].rearrange("p (m n) -> p m n", m=H), ALU.subtract).then_inc(k_diff, 1)
                    dve.wait_ge(k_diff, 1)
                    near = hT[:, 0, 0:D]
                    dve.tensor_scalar(near, pre[:, :], -TOL, None, ALU.is_ge).then_inc(k_diff, 1)
                    dve.wait_ge(k_diff, 2)
                    dve.scalar_tensor_tensor(pre[:, :], pre[:, :], TOL, near, ALU.is_le, ALU.mult).then_inc(k_diff, 1)
                    dve.wait_ge(k_diff, 3)
                    dve.reduce_sum(cnt[:, :], pre[:, :], AX.X).then_inc(k_diff, 1)
                if ref == PAIRS + 3 + GROUP - 2:
                    dve.wait_ge(k_sum, 1)
                    dve.tensor_scalar(miss[:, :], psR[0:1, 0:1], P * D - 0.5, float(K), ALU.is_lt, ALU.mult).then_inc(k_diff, 1)
                    dve.wait_ge(k_diff, 5)
                    dve.tensor_copy(again[:, :], miss[:, :]).then_inc(k_flag, 1)

            def body():
                dve.tensor_copy(hs[:, 1, :, :], h_skip[:, :].rearrange("p (m n) -> p m n", m=H)).then_inc(a_end, 1)
                walk(dve, RUNS1, unit1)
                dve.wait_ge(a_tanh, 4 * RP1)
                dve.tensor_copy(h_end[:, :].rearrange("p (m n) -> p m n", m=H), hs[:, 1, :, :]).then_inc(a_end, 1)
                dve.wait_ge(a_end, 2)
                to = hs[:, 1, :, :].rearrange("p m (b k) -> p (m b) k", b=NB)
                dve.tensor_copy(to[:, :, 1:K], h_end[:, :].rearrange("p (m k) -> p m k", k=K)[:, :, 0:K - 1]).then_inc(a_end, 1)
                dve.memset(to[:, :, 0:1], 0.0).then_inc(a_end, 1)
                dve.wait_ge(a_xb, PAIRS)
                walk(dve, RUNS2, unit2)

            rounds(dve, body, "dve")

        @block.tensor
        def _(pe):
            pe.wait_ge(q_ident, 6)
            pe.wait_ge(q_silu, 1)
            for k in range(H):
                last = pe.transpose(psR[:, k * NB:(k + 1) * NB], csig[:, k * P:(k + 1) * P], ident[0:NB, 0:NB])
            last.then_inc(q_scTp, 1)
            pe.wait_ge(q_scT, 2)
            pe.wait_ge(q_small, 16 * 8)
            for j, ps in enumerate((psC, psT, psO)):
                for k in range(H):
                    last = pe.matmul(ps[:, :], scE[:, k, :, :].rearrange("p b n -> p (b n)"), wm[:, k, j * W:(j + 1) * W],
                                     start=(k == 0), stop=(k == H - 1))
                last.then_inc(q_mod, 1)
            for m in range(H):
                for k in range(H):
                    last = pe.matmul(psW[:, m * NB:(m + 1) * NB], wm[:, k, 5 * D + m * P:5 * D + (m + 1) * P], scT[:, k, :],
                                     start=(k == 0), stop=(k == H - 1))
            last.then_inc(q_mod, 1)
            for n, name in enumerate(NAMES):
                pe.wait_ge(q_w[name], 16)
                ps = (psF, psI, psG)[n % 3]
                if n >= 3:
                    pe.wait_ge(q_act, n - 2)
                    before = sum(x in SPLIT for x in NAMES[:n - 2])
                    if before:
                        pe.wait_ge(q_dve, before)
                for k in range(H):
                    for m in range(H):
                        last = pe.transpose(ps[:, k * D + m * P:k * D + (m + 1) * P], raw[name][:, m, k * P:(k + 1) * P],
                                            ident[:, :])
                last.then_inc(q_pe, 1)
            pe.wait_ge(q_ready, 1)

            def recur(sem_in, sem_free, sem_out, v, tt, back, first, apart):
                for k in range(H):
                    if not first:
                        pe.wait_ge(sem_in, v.lin(4, -4 * back + 2 * tt - 1 + k))
                    for m in range(H):
                        if k == 0 and m == 1 and apart and not first:
                            pe.wait_ge(sem_free, v.lin(4, -4 * back + 2 * tt))
                        ps = (psR, psF)[m][:, 0:P] if apart else psR[:, m * P:(m + 1) * P]
                        ins = pe.matmul(ps, AT[:, k, m * P:(m + 1) * P], hs[:, 1 - tt, k, :],
                                        start=(k == 0 and (apart or m == 0)), stop=(k == H - 1 and (apart or m == H - 1)),
                                        skip_group_check=True)
                        if k == H - 1 and apart:
                            ins.then_inc(sem_out, 1)
                if not apart:
                    ins.then_inc(sem_out, H)

            def unit1(v, ref):
                rec = has(ref, R1LAG, RP1)
                if rec:
                    if ref == R1LAG:
                        pe.wait_ge(a_end, 1)
                    recur(a_tanh, a_pre, a_r, v, 0, R1LAG, ref == R1LAG, True)
                if has(ref, 2, PAIRS):
                    pe.wait_ge(a_h, v.lin(2, -2))
                    if ref >= 3:
                        pe.wait_ge(a_hT, v.lin(1, -2))
                    for tt in range(2):
                        for m in range(H):
                            last = pe.transpose(psT[:, m * 2 * P + tt * P:m * 2 * P + (tt + 1) * P],
                                                htok[:, ref % 2, tt * D + m * P:tt * D + (m + 1) * P], ident[:, :])
                    last.then_inc(a_T, 1)
                if rec:
                    recur(a_tanh, a_pre, a_r, v, 1, R1LAG, False, True)
                if has(ref, 3, PAIRS):
                    pe.wait_ge(a_hT, v.lin(1, -2))
                    if ref >= 4:
                        pe.wait_ge(a_xb, v.lin(1, -3))
                    h = hT[:, (ref - 3) % 2, :].rearrange("p (k n) -> p k n", k=H)
                    for m in range(H):
                        for k in range(H):
                            last = pe.matmul(psB[:, m * 2 * P:(m + 1) * 2 * P], BT[:, k, m * P:(m + 1) * P], h[:, k, :],
                                             start=(k == 0), stop=(k == H - 1))
                    last.then_inc(a_B, 1)

            def split3(ps, name, xhi, xlo, start, stop):
                n = 0
                for m in range(H):
                    for k in range(H):
                        for w, xx in ((whi, xhi), (whi, xlo), (wlo, xhi)):
                            n += 1
                            last = pe.matmul(ps[:, m * GC:(m + 1) * GC], w[name][:, k, m * P:(m + 1) * P], xx(k),
                                             start=(start and n == 1), stop=(stop and n == 6 * H), skip_group_check=True)
                return last

            def unit2(v, ref):
                rec, gates = has(ref, 0, PAIRS), has(ref, G0, PAIRS)
                g, b = grp(ref), v.lin(1, -G0 - GROUP * grp(ref))

                def project(tt):
                    for k in range(H):
                        last = pe.matmul(psC[:, tt * D:(tt + 1) * D], hs[:, tt, k, :], CT[:, k, :],
                                         start=(k == 0), stop=(k == H - 1))
                    return last

                def gate_x(n):
                    if not gates:
                        return
                    if n == 0 and pos(ref) == 0:
                        pe.wait_ge(s_hi, 2 * GROUP * (g + 1))
                        pe.wait_ge(s_lo, 2 * GROUP * (g + 1))
                    if ref > G0:
                        pe.wait_ge((s_f, s_i, s_g)[n], v.lin(2, -2 * G0))
                    split3((psF, psI, psG)[n], ("wf", "wi", "wc")[n],
                           lambda k: hi[:, g % 2, k, bass.ds(b, 1), :].rearrange("p o n -> p (o n)"),
                           lambda k: lo[:, g % 2, k, bass.ds(b, 1), :].rearrange("p o n -> p (o n)"), True, False)

                def gate_c(n):
                    if not gates:
                        return
                    if pos(ref) == 0:
                        xhi, xlo = (lambda k: c0hi[:, k:k + 1].broadcast_to([P, GC])), (lambda k: c0lo[:, k:k + 1].broadcast_to([P, GC]))
                    else:
                        xhi, xlo = (lambda k: chi[:, k, :]), (lambda k: clo[:, k, :])
                        if n == 0:
                            pe.wait_ge(s_chi, v.lin(1, -G0 - g))
                            pe.wait_ge(s_clo, v.lin(1, -G0 - g))
                    split3((psF, psI, psG)[n], ("uf", "ui", "uc")[n], xhi, xlo, False, True).then_inc(s_gate, 1)

                if rec:
                    if ref == 0:
                        pe.wait_ge(a_end, 4)
                    recur(s_tanh, s_pre, s_r, v, 0, 0, ref == 0, ref < G0)
                if has(ref, 1, PAIRS):
                    if not rec:
                        pe.wait_ge(s_tanh, 4 * PAIRS)
                    project(1).then_inc(s_C, 1)
                if has(ref, O0, PAIRS):
                    if ref > O0:
                        pe.wait_ge(s_ws, v.lin(2, -2 * O0))
                    og = (ref - O0) // GROUP
                    p = v.lin(1, -O0 - GROUP * og)
                    split3(psW, "wo", lambda k: hi[:, og % 2, k, :, bass.ds(p * (2 * K), 2 * K)],
                           lambda k: lo[:, og % 2, k, :, bass.ds(p * (2 * K), 2 * K)], True, True).then_inc(s_W, 1)
                if has(ref, 2, PAIRS):
                    pe.wait_ge(s_h2, v.lin(2, -2))
                    if ref > 2:
                        pe.wait_ge(s_hi, v.lin(2, -4))
                        pe.wait_ge(s_lo, v.lin(2, -4))
                    for tt in range(2):
                        for m in range(H):
                            last = pe.transpose(psT[:, m * 2 * P + tt * P:m * 2 * P + (tt + 1) * P],
                                                h2tok[:, tt * D + m * P:tt * D + (m + 1) * P], ident[:, :])
                    last.then_inc(s_T, 1)
                if has(ref, O0 + 1, PAIRS):
                    pe.wait_ge(s_ob, v.lin(2, -2 * O0))
                    if ref > O0 + 1:
                        pe.wait_ge(s_fin, v.lin(1, -O0 - 1))
                    for tt in range(2):
                        for m in range(H):
                            last = pe.transpose(psO[:, tt * D + m * P:tt * D + (m + 1) * P],
                                                ow[:, m * GC + tt * P:m * GC + (tt + 1) * P], ident[:, :])
                    last.then_inc(s_TO, 1)
                if has(ref, O0, PAIRS) and pos(ref) == 0:
                    pe.wait_ge(s_c, ref - G0)
                    pe.wait_ge(s_y, min(ref, PAIRS))
                    for m in range(H):
                        for k in range(H):
                            last = pe.matmul(psC[:, m * GC:(m + 1) * GC], uoT[:, k, m * P:(m + 1) * P], cst[:, k, :],
                                             start=(k == 0), stop=(k == H - 1))
                    last.then_inc(s_U, 1)
                gate_x(0)
                if rec:
                    recur(s_tanh, s_pre, s_r, v, 1, 0, False, ref < G0)
                if ref == PAIRS + 2:
                    pe.wait_ge(k_diff, 4)
                    pe.matmul(psR[0:1, 0:1], cnt[:, :], ones[:, :], start=True, stop=True).then_inc(k_sum, 1)
                gate_x(1)
                gate_x(2)
                if rec:
                    if ref >= 1:
                        pe.wait_ge(s_y, v.lin(1))
                    if has(ref, O0, PAIRS) and pos(ref) == 0:
                        pe.wait_ge(s_u, 2 * ((ref - O0) // GROUP + 1))
                    project(0)
                gate_c(0)
                gate_c(1)
                gate_c(2)

            def body():
                walk(pe, RUNS1, unit1)
                walk(pe, RUNS2, unit2)

            rounds(pe, body, "pe")


_INS = ["L0_attn_x", "L0_attn_A", "L0_attn_B", "L0_attn_C", "L0_attn_gamma", "L0_attn_beta",
        "L0_ffn_wf", "L0_ffn_uf", "L0_ffn_bf", "L0_ffn_wi", "L0_ffn_ui", "L0_ffn_bi", "L0_ffn_wc", "L0_ffn_uc",
        "L0_ffn_bc", "L0_ffn_wo", "L0_ffn_uo", "L0_ffn_bo", "L0_ffn_in_c", "L0_c", "L0_wmod"]


def kernel(**inputs):
    import numpy as _np
    import concourse.bacc as _bacc
    from concourse import mybir as _mybir
    from concourse.bass_utils import run_bass_kernel_spmd as _run

    nc = _bacc.Bacc("TRN2", target_bir_lowering=False, num_devices=1)
    arrays, args = {}, []
    for name in _INS:
        a = _np.ascontiguousarray(inputs[name])
        arrays[f"in_{name}_dram"] = a
        args.append(nc.dram_tensor(f"in_{name}_dram", a.shape, _mybir.dt.from_np(a.dtype), kind="ExternalInput").ap())
    shape = inputs["L0_attn_x"].shape
    args.append(nc.dram_tensor("out_0_dram", shape, _mybir.dt.float32, kind="ExternalOutput").ap())
    adaln_kernel(nc, *args)
    r = _run(nc, [arrays], core_ids=[0])
    return r.results[0]["out_0_dram"]
```

```python
import concourse.bass as bass
from concourse import mybir
from contextlib import ExitStack



class At:

    def __init__(self, i, c):
        self.i, self.c = i, c

    def lin(self, k, c0=0):
        c = k * self.c + c0
        return c if isinstance(self.i, int) else self.i * (2 * k) + c

    def half(self, k, back, c0=0):
        c = k * ((self.c - back) // 2) + c0
        return c if isinstance(self.i, int) else self.i * k + c


def adaln_kernel(nc, x, A, B, C, gamma, beta, wf, uf, bf, wi, ui, bi, wc, uc, bc, wo, uo, bo, in_c, cond, wmod, out):
    f32 = mybir.dt.float32
    f32r = mybir.dt.float32r
    i32 = mybir.dt.int32
    ALU = mybir.AluOpType
    ACT = mybir.ActivationFunctionType
    AX = mybir.AxisListType

    P = 128
    NB, S, D = x.shape
    K = P // NB
    L = S // K
    H = D // P
    SKIP = 8
    PAIRS = L // 2
    SP0 = SKIP // 2
    RP1 = PAIRS - SP0
    W = 2 * D
    GROUP = 8
    NG = PAIRS // GROUP
    GC = 2 * GROUP * K
    RING = 2 * GROUP
    EPS = 1e-5
    TOL = 2.0 ** -18

    G0 = GROUP + 3
    O0 = G0 + GROUP
    UNITS2 = O0 + PAIRS + 1
    TAIL = G0 + PAIRS
    CS = G0 - 1
    R1LAG = 6
    UNITS1 = PAIRS + 4
    RAW = 8
    LATE = ["wf", "wi", "wc", "uf", "ui", "uc", "wo", "uo"]
    LOADS = {1: ["B", "A", "wmod", "C"], 2: ["affine"], 3: ["wf"], 4: ["wi"], 5: ["wc"], 6: ["bias"]}

    x_v = x.rearrange("b (k t) d -> (b k) (t d)", k=K)
    out_v = out.rearrange("b (k t) d -> (b k) (t d)", k=K)
    wmod_v = wmod.rearrange("(k p) n -> p k n", p=P)
    h_park = nc.dram_tensor("h_park", [PAIRS, P, W], f32, kind="Internal").ap()

    ctx = ExitStack()
    with ctx:
        def sb(name, shape, dt=f32):
            return ctx.enter_context(nc.sbuf_tensor(name, shape, dt))

        def sem(name):
            return ctx.enter_context(nc.semaphore(name))

        ident = sb("ident", [P, P])
        ones = sb("ones", [P, 1])
        mhalf = sb("mhalf", [P, 2])
        epst = sb("epst", [P, 2])
        AT = sb("AT", [P, H, D])
        uoT = sb("uoT", [P, H, D])
        SPLIT = ["C", "wf", "wi", "wc", "uf", "ui", "uc", "wo"]
        whi = {n: sb(n + "T_hi", [P, H, D], f32r) for n in SPLIT}
        wlo = {n: sb(n + "T_lo", [P, H, D], f32r) for n in SPLIT}
        gag = sb("gag", [P, D])
        gab = sb("gab", [P, D])
        cb1 = sb("cb1", [P, D])
        sbt = sb("sbt", [P, D])
        gbT = sb("gbT", [P, H, NB])
        bias = sb("bias", [P, 4, H])
        c0 = sb("c0", [P, H])
        c0hi = sb("c0hi", [P, H], f32r)
        c0lo = sb("c0lo", [P, H], f32r)

        state = sb("state", [P, PAIRS * W])
        hi = sb("hi", [P, 2, H, NB, GC], f32r)
        lo = sb("lo", [P, 2, H, NB, GC], f32r)
        xin = sb("xin", [P, 2, W])
        htok = sb("htok", [P, 2, W])
        h2tok = sb("h2tok", [P, W])
        y = sb("y", [P, W])[:, :]
        ow = sb("ow", [P, W])[:, :]
        pre = sb("pre", [P, D])
        hs = sb("hs", [P, 2, H, P])
        hs_hi = sb("hs_hi", [P, 2, H, P], f32r)
        hs_lo = sb("hs_lo", [P, 2, H, P], f32r)
        h_skip = sb("h_skip", [P, D])
        h_end = sb("h_end", [P, D])
        gf = sb("gf", [P, H, GC])
        gi = sb("gi", [P, H, GC])
        gg = sb("gg", [P, H, GC])
        cst = sb("cst", [P, H, GC])
        chi = sb("chi", [P, H, GC], f32r)
        clo = sb("clo", [P, H, GC], f32r)
        uvec = sb("uvec", [P, H, GC])
        whi["B"], wlo["B"] = chi, clo
        ca1, sa = uvec[:, 0, :], uvec[:, 1, :]
        hmT_hi, hmT_lo = (r[:, 0, 0, 0:4, :].rearrange("p (i c) n -> p i (c n)", i=2) for r in (hi, lo))
        st = sb("st", [P, 2, 6])
        stb = sb("stb", [P, 2, 6])
        mv = sb("mv", [P, 2, 2])
        mvb = sb("mvb", [P, 2, 2])
        ve = sb("ve", [P, 2])
        rstd = sb("rstd", [P, 2])
        rstdb = sb("rstdb", [P, 2])
        cnt = sb("cnt", [P, 1])
        miss = sb("miss", [1, 1])
        again = sb("again", [1, 1], i32)

        EARLY = ["B", "A", "C"]
        NAMES = EARLY + LATE
        at = RAW * W
        raw = {n: state[:, at + i * W:at + (i + 1) * W].rearrange("p (m d) -> p m d", m=H) for i, n in enumerate(EARLY)}
        at += len(EARLY) * W
        for i, n in enumerate(LATE):
            raw[n] = (gf, gi, gg)[i % 3][:, :, :]
        wm = [state[:, at + 2 * j * W:at + 2 * (j + 1) * W].rearrange("p (k n) -> p k n", k=H) for j in range(3)]
        at += 6 * W
        gamma_b = state[:, at:at + D]
        beta_b = state[:, at + D:at + 2 * D]
        cn = state[0:NB, at + W:at + W + D]
        csig = state[0:NB, at + W + D:at + 2 * W]
        at += 2 * W
        scT = state[:, at:at + H * NB].rearrange("p (k b) -> p k b", k=H)
        scE = state[:, at + D:at + D + H * P].rearrange("p (k b n) -> p k b n", k=H, b=NB)
        at += W
        ga = state[:, at:at + D]
        gmag = state[:, at + D:at + 2 * D]
        gs = state[:, at + 2 * D:at + 2 * D + H * NB].rearrange("p (k b) -> p k b", k=H)
        gm = state[:, at + 3 * D:at + 3 * D + H * NB].rearrange("p (k b) -> p k b", k=H)

        def bank(name):
            return ctx.enter_context(nc.psum_tensor(name, [P, 512], f32))

        psR, psC, psT, psF, psI, psG, psW, psO = (bank(n) for n in (
            "psR", "psC", "psT", "psF", "psI", "psG", "psW", "psO"))
        psB = psW
        BANK = dict(zip(NAMES, (psI, psG, psI, psG, psO, psI, psG, psO, psI, psG, psO)))

        def place(name):
            n = NAMES.index(name)
            before = [x for x in range(n) if BANK[NAMES[x]] is BANK[name]]
            last = before[-1] if before else None
            return n, last, sum(x in whi for x in NAMES[:last + 1]) if before else 0


        def nth_split(name):
            return sum(x in whi for x in NAMES[:NAMES.index(name)])

        def whole(name):
            if name == "B":
                return state[:, 0:W].rearrange("p (k d) -> p k d", k=H)
            if name == "C":
                return ow.rearrange("p (k d) -> p k d", k=H)
            return (cst, uvec)[LATE.index(name) % 2][:, :, :]

        def two(u, one, other):
            return other if u >= TAIL and u % 2 == TAIL % 2 else one

        def ow_of(u):
            return two(u, ow, y)

        def psW_of(u):
            return two(u, psW, psF)

        def psO_of(u):
            return two(u, psO, psI)

        q_ident = sem("q_ident")
        q_table = sem("q_table")
        q_w = {n: sem("q_w_" + n) for n in NAMES}
        q_wm = [sem(f"q_wm{j}") for j in range(3)]
        q_cond = sem("q_cond")
        q_affine = sem("q_affine")
        q_bias = sem("q_bias")
        q_wT = sem("q_wT")
        q_whi = sem("q_whi")
        q_wcopy = sem("q_wcopy")
        q_wlo = sem("q_wlo")
        q_sig = sem("q_sig")
        q_silu = sem("q_silu")
        q_scTp = sem("q_scTp")
        q_scT = sem("q_scT")
        q_mod = sem("q_mod")
        q_tab = sem("q_tab")
        q_tables = sem("q_tables")
        a_x = [sem(f"a_xin{i}") for i in range(2)]
        a_stats = sem("a_stats")
        a_mv = sem("a_mv")
        a_ve = sem("a_ve")
        a_rstd = sem("a_rstd")
        a_tmp = sem("a_tmp")
        a_h = sem("a_h")
        a_park = [sem(f"a_park{i}") for i in range(2)]
        a_T = sem("a_T")
        a_hT = sem("a_hT")
        a_hl = sem("a_hl")
        a_sc = sem("a_sc")
        a_B = sem("a_B")
        a_xb = sem("a_xb")
        a_r = sem("a_r")
        a_pre = sem("a_pre")
        a_tanh = sem("a_tanh")
        a_end = sem("a_end")
        s_x = [sem(f"s_xin{i}") for i in range(2)]
        s_h = [sem(f"s_hin{i}") for i in range(2)]
        s_r = sem("s_r")
        s_pre = sem("s_pre")
        s_tanh = sem("s_tanh")
        s_hsh = sem("s_hsh")
        s_hsl = sem("s_hsl")
        s_skip = sem("s_skip")
        s_C = sem("s_C")
        s_y = sem("s_y")
        s_stA = sem("s_stA")
        s_mvA = sem("s_mvA")
        s_veA = sem("s_veA")
        s_rA = sem("s_rA")
        s_tmpA = sem("s_tmpA")
        s_xg = sem("s_xg")
        s_x1 = sem("s_x1")
        s_stB = sem("s_stB")
        s_mvB = sem("s_mvB")
        s_veB = sem("s_veB")
        s_rB = sem("s_rB")
        s_tmpB = sem("s_tmpB")
        s_scB = sem("s_scB")
        s_h2 = sem("s_h2")
        s_T = sem("s_T")
        s_hi = sem("s_hi")
        s_lo = sem("s_lo")
        s_gate = sem("s_gate")
        s_f = sem("s_f")
        s_i = sem("s_i")
        s_g = sem("s_g")
        s_fc = sem("s_fc")
        s_ig = sem("s_ig")
        s_c = sem("s_c")
        s_chi = sem("s_chi")
        s_clo = sem("s_clo")
        s_U = sem("s_U")
        s_u = sem("s_u")
        s_W = sem("s_W")
        s_ws = sem("s_ws")
        s_ot = sem("s_ot")
        s_ob = sem("s_ob")
        s_TO = sem("s_TO")
        s_fin = sem("s_fin")
        s_out = sem("s_out")
        k_diff = sem("k_diff")
        k_sum = sem("k_sum")
        k_flag = sem("k_flag")
        s_apart = sem("s_apart")
        per_round = [*q_w.values(), *q_wm, q_cond, q_affine, q_bias, q_wT, q_whi, q_wcopy, q_wlo, q_sig, q_silu, q_scTp,
                     q_scT, q_mod, q_tab, q_tables, *a_x, a_stats, a_mv, a_ve, a_rstd, a_tmp, a_h, *a_park, a_T, a_hT, a_hl, a_sc, a_B, a_xb, a_r, a_pre,
                     a_tanh, a_end, *s_x, *s_h, s_r, s_pre, s_tanh, s_hsh, s_hsl, s_skip, s_C, s_y, s_stA, s_mvA, s_veA, s_rA,
                     s_tmpA, s_xg, s_x1, s_stB, s_mvB, s_veB, s_rB, s_tmpB, s_scB, s_h2, s_T, s_hi, s_lo, s_gate, s_f,
                     s_i, s_g, s_fc, s_ig, s_c, s_chi, s_clo, s_U, s_u, s_W, s_ws, s_ot, s_ob, s_TO, s_fin,
                     s_out, k_diff, k_sum, k_flag, s_apart]
        r_over = sem("r_over")
        r_next = sem("r_next")

        def ranges(cuts, end):
            return list(zip(cuts, cuts[1:] + [end]))

        RUNS1 = ranges([*range(max(LOADS) + 2), RP1, RP1 + 1, RP1 + 2, RP1 + 3, RP1 + 4, RP1 + 5, RP1 + 6], UNITS1)
        cuts = {*range(G0 + 1), PAIRS, PAIRS + 1, PAIRS + 2, PAIRS + 3, O0 + 1, O0 + 2, UNITS2 - 1}
        for g in range(NG + 1):
            cuts |= {G0 + GROUP * g, G0 + GROUP * g + 1, G0 + GROUP * g - 1}
        RUNS2 = ranges(sorted(c for c in cuts if c < UNITS2), UNITS2)

        def walk(eng, runs, unit):
            for a, b in runs:
                n = (b - a) // 2
                if n < 2:
                    n = 0
                if n:
                    with eng.Fori(0, n) as i:
                        unit(At(i, a), a)
                        unit(At(i, a + 1), a + 1)
                for c in range(a + 2 * n, b):
                    unit(At(0, c), c)

        def pair1(v, ref, back):
            return v.lin(1, SP0 - back) if ref - back < RP1 else v.lin(1, -RP1 - back)

        def has(ref, first, n):
            return first <= ref < first + n

        def grp(ref):
            return (ref - G0) // GROUP

        def pos(ref):
            return (ref - G0) % GROUP

        def row(v, k, off=0, n=W):
            return state[:, bass.ds(v * W + off, n)] if not isinstance(v, int) else state[:, v * W + off:v * W + off + n]

        def tposed(m):
            return psT[:, m * 2 * P:(m + 1) * 2 * P].rearrange("p (t b k) -> p t b k", t=2, b=NB)

        def ring(buf, v, ref, back, m):
            g, p = (ref - back) // GROUP, v.lin(1, -back - GROUP * ((ref - back) // GROUP))
            part = buf[:, g % 2, m, :, bass.ds(p * (2 * K), 2 * K)]
            return part.rearrange("p b (t k) -> p t b k", t=2)

        def apart(eng):
            eng.sem_inc(s_apart, 1)

        def rounds(eng, body, name):
            left = eng.alloc_register("rounds_" + name)
            eng.reg_mov(left, K)
            with eng.Fori(0, left) as r:
                body()
                eng.wait_ge(k_flag, 1)
                eng.reg_mov(left, eng.value_load(again[0:1, 0:1], min_val=0, max_val=K))
                eng.drain().then_inc(r_over, 1)
                eng.wait_ge(r_next, r + 1)

        block = ctx.enter_context(nc.Block())

        @block.sync
        def _(sp):
            weights = dict(zip(("A", "B", "C", "wf", "wi", "wc", "uf", "ui", "uc", "wo", "uo"),
                               (A, B, C, wf, wi, wc, uf, ui, uc, wo, uo)))
            def load(what):
                if what == "wmod":
                    for j in (1, 2):
                        sp.dma_start(wm[j], wmod_v[:, :, j * W:(j + 1) * W]).then_inc(q_wm[j], 16)
                elif what == "affine":
                    for dst, src in ((gamma_b, gamma), (beta_b, beta)):
                        sp.dma_start(dst, src.rearrange("(o n) -> o n", o=1).broadcast_to([P, D])).then_inc(q_affine, 16)
                elif what == "bias":
                    for j, src in enumerate((bf, bi, bc, bo)):
                        sp.dma_start(bias[:, j, :], src.rearrange("(m p) -> p m", p=P),
                                     allow_slow_non_contiguous=True).then_inc(q_bias, 16)
                    sp.dma_start(c0[:, :], in_c.rearrange("(m p) -> p m", p=P),
                                 allow_slow_non_contiguous=True).then_inc(q_bias, 16)
                else:
                    sp.dma_start(raw[what], weights[what].rearrange("(m p) d -> p m d", p=P)).then_inc(q_w[what], 16)

            def unit1(v, ref):
                if has(ref, 0, PAIRS):
                    if ref >= 2:
                        sp.wait_ge(a_tmp, v.lin(2, -2))
                    p = pair1(v, ref, 0)
                    sp.dma_start(xin[:, ref % 2, :], x_v[:, bass.ds(p * W, W)]).then_inc(a_x[ref % 2], 16)
                if has(ref, 2, PAIRS):
                    sp.wait_ge(a_h, v.lin(2, -2))
                    p = pair1(v, ref, 2)
                    sp.dma_start(h_park[bass.ds(p, 1), :, :].rearrange("o p w -> p (o w)"),
                                 htok[:, ref % 2, :]).then_inc(a_park[ref % 2], 16)
                for what in LOADS.get(ref, []):
                    load(what)

            def unit2(v, ref):
                if has(ref, 0, PAIRS):
                    if ref >= 2:
                        sp.wait_ge(s_x1, v.lin(2, -2))
                    sp.dma_start(xin[:, ref % 2, :], x_v[:, bass.ds(v.lin(W), W)]).then_inc(s_x[ref % 2], 16)
                    sp.dma_start(htok[:, ref % 2, :],
                                 h_park[bass.ds(v.lin(1), 1), :, :].rearrange("o p w -> p (o w)")).then_inc(s_h[ref % 2], 16)
                if 1 <= ref < len(LATE) - 2:
                    sp.wait_ge(q_wT, len(EARLY) + ref)
                    load(LATE[ref + 2])
                if has(ref, O0 + 1, PAIRS):
                    sp.wait_ge(s_fin, v.lin(1, -O0))
                    sp.dma_start(out_v[:, bass.ds(v.lin(W, -(O0 + 1) * W), W)], row(v.lin(1, -O0 - 1), 1)).then_inc(s_out, 16)

            left = sp.alloc_register("rounds_sp")
            sp.reg_mov(left, K)
            with sp.Fori(0, left) as r:
                sp.dma_start(cn, cond).then_inc(q_cond, 16)
                sp.dma_start(wm[0], wmod_v[:, :, 0:W]).then_inc(q_wm[0], 16)
                walk(sp, RUNS1, unit1)
                sp.wait_ge(a_park[0], 16 * (PAIRS // 2))
                sp.wait_ge(a_park[1], 16 * (PAIRS // 2))
                sp.wait_ge(a_T, PAIRS)
                walk(sp, RUNS2, unit2)
                sp.wait_ge(s_out, 16 * PAIRS)
                sp.wait_ge(k_flag, 1)
                sp.reg_mov(left, sp.value_load(again[0:1, 0:1], min_val=0, max_val=K))
                sp.wait_ge(r_over, r * 4 + 4)
                apart(sp)
                for s in per_round:
                    sp.sem_clear(s)
                sp.sem_inc(r_next, 1)

        @block.gpsimd
        def _(pool):
            pool.memset(ident[:, :], 0.0).then_inc(q_ident, 1)
            pool.wait_ge(q_ident, 1)
            pool.affine_select(out=ident[:, :], in_=ident[:, :], compare_op=ALU.not_equal, fill=1.0, base=0,
                               pattern=[[-1, P]], channel_multiplier=1).then_inc(q_ident, 1)
            pool.memset(mhalf[:, :], -0.5).then_inc(q_ident, 1)
            pool.memset(ones[:, :], 1.0).then_inc(q_ident, 1)
            pool.memset(epst[:, :], EPS).then_inc(q_ident, 1)
            pool.memset(h_skip[:, :], 0.0).then_inc(q_ident, 1)
            pool.wait_ge(q_ident, 6)
            def weight(name):
                if name in whi:
                    pool.wait_ge(q_wcopy, nth_split(name) + 1)
                    pool.wait_ge(q_whi, NAMES.index(name) + 1)
                    pool.tensor_tensor(wlo[name][:, :, :], whole(name), whi[name][:, :, :].bitcast(f32),
                                       ALU.subtract).then_inc(q_wlo, 1)

            def unit1(v, ref):
                if ref == 1:
                    weight("B")
                if has(ref, 1, PAIRS):
                    pool.wait_ge(a_mv, v.lin(2))
                    pool.tensor_tensor(ve[:, :], mv[:, :, 1], epst[:, :], ALU.add).then_inc(a_ve, 1)
                    pool.wait_ge(a_ve, v.lin(1))
                    pool.tensor_tensor(rstd[:, :], ve[:, :], mhalf[:, :], ALU.pow).then_inc(a_rstd, 1)
                    if ref == 1:
                        pool.wait_ge(q_tab, 2)
                    for tt in range(2):
                        pool.wait_ge(a_sc, v.lin(2, tt - 1))
                        h = htok[:, (ref - 1) % 2, tt * D:(tt + 1) * D]
                        pool.tensor_tensor(h, h, sa, ALU.add).then_inc(a_h, 1)
                if ref == 2:
                    weight("C")

            def state_low(v, tt):
                pool.wait_ge(s_hsh, v.lin(2, -2 * CS + tt + 1))
                pool.tensor_tensor(hs_lo[:, tt, :, :], hs[:, tt, :, :], hs_hi[:, tt, :, :].bitcast(f32),
                                   ALU.subtract).then_inc(s_hsl, 1)

            def unit2(v, ref):
                if has(ref, 3, PAIRS):
                    pool.wait_ge(s_scB, v.lin(2, -4))
                    h2 = h2tok[:, :].rearrange("p (t d) -> p t d", t=2)
                    pool.tensor_tensor(h2, h2, sbt[:, :].rearrange("p (o d) -> p o d", o=1).broadcast_to([P, 2, D]),
                                       ALU.add).then_inc(s_h2, 1)
                if has(ref, G0 + 1, PAIRS):
                    pool.wait_ge(s_i, v.lin(2, -2 * G0))
                    pool.wait_ge(s_g, v.lin(2, -2 * G0))
                    pool.tensor_tensor(gi[:, :, :], gi[:, :, :], gg[:, :, :], ALU.mult).then_inc(s_ig, 1)
                if has(ref, CS, PAIRS - CS):
                    state_low(v, 0)
                if has(ref, 1, PAIRS):
                    pool.wait_ge(s_x[(ref - 1) % 2], v.half(16, 1, 16))
                    xg = xin[:, (ref - 1) % 2, :].rearrange("p (t d) -> p t d", t=2)
                    pool.tensor_tensor(xg, xg, gab[:, :].rearrange("p (o d) -> p o d", o=1).broadcast_to([P, 2, D]),
                                       ALU.add).then_inc(s_xg, 1)
                if has(ref, 2, PAIRS):
                    pool.wait_ge(s_mvB, v.lin(2, -2))
                    if ref >= 3:
                        pool.wait_ge(s_rA, v.lin(1, -1))
                    pool.tensor_tensor(ve[:, :], mvb[:, :, 1], epst[:, :], ALU.add).then_inc(s_veB, 1)
                    pool.wait_ge(s_veB, v.lin(1, -1))
                    pool.tensor_tensor(rstdb[:, :], ve[:, :], mhalf[:, :], ALU.pow).then_inc(s_rB, 1)
                if has(ref, 1, PAIRS):
                    pool.wait_ge(s_mvA, v.lin(2))
                    if ref >= 2:
                        pool.wait_ge(s_rB, v.lin(1, -1))
                    pool.tensor_tensor(ve[:, :], mv[:, :, 1], epst[:, :], ALU.add).then_inc(s_veA, 1)
                    pool.wait_ge(s_veA, v.lin(1))
                    pool.tensor_tensor(rstd[:, :], ve[:, :], mhalf[:, :], ALU.pow).then_inc(s_rA, 1)
                if has(ref, CS, PAIRS - CS):
                    state_low(v, 1)
                if 1 <= ref <= len(LATE):
                    weight(LATE[ref - 1])
                if has(ref, O0, PAIRS):
                    pool.wait_ge(s_ot, v.lin(1, -O0 + 1))
                    for m in range(H):
                        o4 = ow_of(ref)[:, m * GC:(m + 1) * GC].rearrange("p (t b k) -> p t b k", t=2, b=NB)
                        g4 = gbT[:, m:m + 1, :].rearrange("p o (b k) -> p o b k", k=1).broadcast_to([P, 2, NB, K])
                        pool.tensor_tensor(o4, o4, g4, ALU.mult).then_inc(s_ob, 1)

            def body():
                walk(pool, RUNS1, unit1)
                pool.wait_ge(q_tab, 16)
                walk(pool, RUNS2, unit2)

            rounds(pool, body, "pool")

        @block.scalar
        def _(act):
            act.wait_ge(q_ident, 6)
            act.activation(cnt[:, :], ones[:, :], ACT.Sigmoid).then_inc(q_table, 1)
            act.wait_ge(q_table, 1)

            def weight(name):
                act.wait_ge(q_wT, NAMES.index(name) + 1)
                if name in whi:
                    if name in LATE[2:]:
                        act.wait_ge(q_wlo, LATE.index(name) + 1)
                    act.activation(whole(name), BANK[name][:, :].rearrange("p (k d) -> p k d", k=H), ACT.Copy).then_inc(q_wcopy, 1)
                dst = {"A": AT, "uo": uoT}.get(name)
                dst = whi[name] if dst is None else dst
                act.activation(dst[:, :, :], BANK[name][:, :].rearrange("p (k d) -> p k d", k=H), ACT.Copy).then_inc(q_whi, 1)

            def prepare():
                act.wait_ge(q_cond, 16)
                act.activation(csig, cn, ACT.Sigmoid).then_inc(q_sig, 1)
                weight("B")
                weight("A")

            def tanhs(sem_in, sem_out, v, tt, back, apart):
                if not apart:
                    act.wait_ge(sem_in, v.lin(4, -4 * back + 2 * tt + H))
                    act.activation(hs[:, tt, :, :], pre[:, :].rearrange("p (m n) -> p m n", m=H), ACT.Tanh).then_inc(sem_out, H)
                    return
                for m in range(H):
                    act.wait_ge(sem_in, v.lin(4, -4 * back + 2 * tt + m + 1))
                    act.activation(hs[:, tt, m, :], pre[:, m * P:(m + 1) * P], ACT.Tanh).then_inc(sem_out, 1)

            def unit1(v, ref):
                rec = has(ref, R1LAG, RP1)
                if rec:
                    tanhs(a_pre, a_tanh, v, 0, R1LAG, True)
                if has(ref, 3, PAIRS):
                    act.wait_ge(a_T, v.lin(1, -2))
                    if ref >= 5:
                        act.wait_ge(a_B, v.lin(1, -4))
                    act.activation(hmT_hi[:, (ref - 3) % 2, :], (psT, psC)[(ref - 3) % 2][:, :], ACT.Copy).then_inc(a_hT, 1)
                if rec:
                    tanhs(a_pre, a_tanh, v, 1, R1LAG, True)
                if has(ref, 4, PAIRS):
                    act.wait_ge(a_B, v.lin(1, -3))
                    act.activation(row(pair1(v, ref, 4), 1), psB[:, :], ACT.Copy).then_inc(a_xb, 1)
                if has(ref, 1, PAIRS):
                    act.wait_ge(a_rstd, v.lin(1))
                    for tt in range(2):
                        act.wait_ge(a_tmp, v.lin(2, tt - 1))
                        h = htok[:, (ref - 1) % 2, tt * D:(tt + 1) * D]
                        act.activation(h, h, ACT.Copy, scale=rstd[:, tt:tt + 1]).then_inc(a_sc, 1)
                if ref == 1:
                    weight("C")

            def state_of(v, ref, tt):
                if ref > CS:
                    act.wait_ge(s_hsl, v.lin(2, -2 * CS + tt - 1))
                tanhs(s_pre, s_tanh, v, tt, 0, ref < G0)
                if ref >= CS:
                    act.wait_ge(s_tanh, v.lin(4, 2 * tt + 2))
                    if ref > CS:
                        act.wait_ge(s_C, v.lin(1))
                    act.activation(hs_hi[:, tt, :, :], hs[:, tt, :, :], ACT.Copy).then_inc(s_hsh, 1)

            def unit2(v, ref):
                if 1 <= ref <= len(LATE):
                    weight(LATE[ref - 1])
                if has(ref, 0, PAIRS):
                    state_of(v, ref, 0)
                if has(ref, G0 + 1, PAIRS) and pos(ref - 1) < GROUP - 1:
                    act.wait_ge(s_c, v.lin(1, -G0))
                    act.activation(chi[:, :, :], cst[:, :, :], ACT.Copy).then_inc(s_chi, 1)
                if has(ref, 3, PAIRS):
                    act.wait_ge(s_T, v.lin(1, -2))
                    for m in range(H):
                        act.activation(ring(hi, v, ref, 3, m), tposed(m), ACT.Copy).then_inc(s_hi, 1)
                if has(ref, 0, PAIRS):
                    state_of(v, ref, 1)
                if has(ref, O0, PAIRS) and pos(ref) == 0:
                    act.wait_ge(s_U, (ref - O0) // GROUP + 1)
                    if ref > O0:
                        act.wait_ge(s_ws, 2 * (ref - O0))
                    for m in range(H):
                        act.activation(uvec[:, m, :], psC[:, m * GC:(m + 1) * GC], ACT.Identity,
                                       bias=bias[:, 3, m:m + 1]).then_inc(s_u, 1)
                if has(ref, 2, PAIRS):
                    act.wait_ge(s_rB, v.lin(1, -1))
                    for tt in range(2):
                        act.wait_ge(s_tmpB, v.lin(2, tt - 3))
                        h2 = h2tok[:, tt * D:(tt + 1) * D]
                        act.activation(h2, h2, ACT.Copy, scale=rstdb[:, tt:tt + 1]).then_inc(s_scB, 1)
                if has(ref, O0, PAIRS):
                    act.wait_ge(s_ws, v.lin(2, -2 * O0 + 2))
                    act.activation(ow_of(ref), ow_of(ref), ACT.Tanh).then_inc(s_ot, 1)
                if has(ref, G0, PAIRS):
                    if ref > G0:
                        act.wait_ge(s_c, v.lin(1, -G0))
                    for n, (dst, src, fn, s) in enumerate(((gf, psF, ACT.Sigmoid, s_f), (gi, psI, ACT.Sigmoid, s_i),
                                                           (gg, psG, ACT.Tanh, s_g))):
                        act.wait_ge(s_gate, v.lin(3, -3 * G0 + n + 1))
                        for m in range(H):
                            act.activation(dst[:, m, :], src[:, m * GC:(m + 1) * GC], fn,
                                           bias=bias[:, n, m:m + 1]).then_inc(s, 1)

            def body():
                prepare()
                walk(act, RUNS1, unit1)
                act.wait_ge(q_bias, 16 * 5)
                walk(act, RUNS2, unit2)

            rounds(act, body, "act")

        @block.vector
        def _(dve):
            dve.wait_ge(q_ident, 6)
            n_tab = [0]

            def halfw(t, tt):
                return t[:, tt * D:(tt + 1) * D]

            def tab(ins):
                n_tab[0] += 1
                ins.then_inc(q_tab, 1)

            def tabs_done():
                dve.wait_ge(q_tab, n_tab[0])

            def prepare():
                dve.wait_ge(q_sig, 1)
                dve.tensor_tensor(csig, cn, csig, ALU.mult).then_inc(q_silu, 1)
                dve.wait_ge(q_scTp, 1)
                dve.tensor_copy(scT, psR[:, 0:H * NB].rearrange("p (k b) -> p k b", k=H)).then_inc(q_scT, 1)
                dve.tensor_copy(scE, psR[:, 0:H * NB].rearrange("p (k b o) -> p k b o", k=H, o=1)
                                .broadcast_to([P, H, NB, K])).then_inc(q_scT, 1)
                dve.wait_ge(a_x[0], 16)
                for tt in range(2):
                    dve.bn_stats(st[:, tt, :], halfw(xin[:, 0, :], tt)).then_inc(a_stats, 1)
                dve.wait_ge(q_mod, 1)
                tab(dve.tensor_scalar(ca1, psC[:, D:W], 1.0, None, ALU.add))
                tab(dve.tensor_copy(sa, psC[:, 0:D]))
                tabs_done()

            def tables():
                dve.wait_ge(q_mod, 4)
                tab(dve.tensor_copy(sbt[:, :], psO[:, D:W]))
                tab(dve.tensor_scalar(cb1[:, :], psF[:, 0:D], 1.0, None, ALU.add))
                gbp = psR[:, D:D + H * NB].rearrange("p (k b) -> p k b", k=H)
                for src, up, down in ((psO[:, 0:D], ga, gmag), (gbp, gs, gm)):
                    tab(dve.tensor_scalar(up, src, 0.25, None, ALU.max))
                    tab(dve.tensor_scalar(down, src, -0.25, None, ALU.min))
                tabs_done()
                for src, up, down in ((psO[:, 0:D], ga, gmag), (gbp, gs, gm)):
                    tab(dve.scalar_tensor_tensor(up, src, 0.0, up, ALU.is_ge, ALU.mult))
                    tab(dve.scalar_tensor_tensor(down, src, 0.0, down, ALU.is_lt, ALU.mult))
                tabs_done()
                tab(dve.tensor_tensor(ga, ga, gmag, ALU.add))
                tab(dve.tensor_tensor(gbT[:, :, :], gs, gm, ALU.add))
                tabs_done()
                dve.wait_ge(q_affine, 16 * 2)
                tab(dve.tensor_tensor(gag[:, :], ga, gamma_b, ALU.mult))
                tab(dve.tensor_tensor(gab[:, :], ga, beta_b, ALU.mult))
                tabs_done()

            def initial():
                dve.wait_ge(q_bias, 16 * 5)
                tab(dve.tensor_copy(c0hi[:, :], c0[:, :]))
                tabs_done()
                dve.tensor_tensor(c0lo[:, :], c0[:, :], c0hi[:, :].bitcast(f32), ALU.subtract).then_inc(q_tables, 1)

            def adds(sem_in, sem_out, v, tt, back, p, apart):
                if not apart:
                    dve.wait_ge(sem_in, v.lin(4, -4 * back + 2 * tt + H))
                    xb = row(p, 1).rearrange("p (m t n) -> p m t n", m=H, t=2)[:, :, tt, :]
                    dve.tensor_tensor(pre[:, :].rearrange("p (m n) -> p m n", m=H),
                                      psR[:, 0:D].rearrange("p (m n) -> p m n", m=H), xb, ALU.add).then_inc(sem_out, H)
                    return
                for m in range(H):
                    dve.wait_ge(sem_in, v.lin(4, -4 * back + 2 * tt + m + 1))
                    xb = row(p, 1, m * 2 * P + tt * P, P)
                    dve.tensor_tensor(pre[:, m * P:(m + 1) * P], (psR, psF)[m][:, 0:P], xb, ALU.add).then_inc(sem_out, 1)

            def unit1(v, ref):
                rec, norm = has(ref, R1LAG, RP1), has(ref, 1, PAIRS)
                src, dst = xin[:, (ref - 1) % 2, :], htok[:, (ref - 1) % 2, :]

                def count(tt):
                    if has(ref, 1, PAIRS - 1):
                        if tt == 0:
                            dve.wait_ge(a_x[ref % 2], v.half(16, 0, 16))
                            dve.wait_ge(a_mv, v.lin(2))
                            apart(dve)
                        dve.bn_stats(st[:, tt, :], halfw(xin[:, ref % 2, :], tt)).then_inc(a_stats, 1)

                if rec:
                    dve.wait_ge(a_xb, v.lin(1, 1 - R1LAG))
                    adds(a_r, a_pre, v, 0, R1LAG, v.lin(1, SP0 - R1LAG), True)
                if norm:
                    dve.wait_ge(a_stats, v.lin(2))
                    if ref >= 2:
                        dve.wait_ge(a_ve, v.lin(1, -1))
                    apart(dve)
                    for tt in range(2):
                        dve.bn_aggr(mv[:, tt, :], st[:, tt, :]).then_inc(a_mv, 1)
                    if ref >= 3:
                        dve.wait_ge(a_T, v.lin(1, -2))
                        dve.wait_ge(a_park[(ref - 1) % 2], v.half(16, 1))
                    for tt in range(2):
                        dve.wait_ge(a_mv, v.lin(2, tt - 1))
                        dve.scalar_tensor_tensor(halfw(dst, tt), halfw(src, tt), mv[:, tt, 0:1], ca1,
                                                 ALU.subtract, ALU.mult).then_inc(a_tmp, 1)
                if rec:
                    adds(a_r, a_pre, v, 1, R1LAG, v.lin(1, SP0 - R1LAG), True)
                if has(ref, 3, PAIRS):
                    dve.wait_ge(a_hT, v.lin(1, -2))
                    dve.tensor_tensor(hmT_lo[:, (ref - 3) % 2, :], (psT, psC)[(ref - 3) % 2][:, :], hmT_hi[:, (ref - 3) % 2, :].bitcast(f32),
                                      ALU.subtract).then_inc(a_hl, 1)
                count(0)
                count(1)
                if ref == 3:
                    tables()

            def unit2(v, ref):
                rec, post, outp = has(ref, 0, PAIRS), has(ref, 1, PAIRS), has(ref, O0, PAIRS)
                bk = (ref - 1) % 2
                if rec:
                    adds(s_r, s_pre, v, 0, 0, v.lin(1), ref < G0)
                if has(ref, G0 + 1, PAIRS):
                    dve.wait_ge(s_fc, v.lin(1, -G0))
                    dve.wait_ge(s_ig, v.lin(1, -G0))
                    dve.tensor_tensor(cst[:, :, :], gf[:, :, :], gi[:, :, :], ALU.add).then_inc(s_c, 1)
                if post:
                    dve.wait_ge(s_C, v.lin(1))
                    dve.wait_ge(s_h[bk], v.half(16, 1, 16))
                    dve.tensor_tensor(y, psC[:, :], htok[:, bk, :], ALU.add).then_inc(s_y, 1)
                if has(ref, G0 + 1, PAIRS) and pos(ref - 1) < GROUP - 1:
                    dve.wait_ge(s_c, v.lin(1, -G0))
                    dve.wait_ge(s_chi, v.lin(1, -G0 - grp(ref - 1)))
                    dve.tensor_tensor(clo[:, :, :], cst[:, :, :], chi[:, :, :].bitcast(f32), ALU.subtract).then_inc(s_clo, 1)
                if has(ref, 2, PAIRS):
                    dve.wait_ge(s_stB, v.lin(2, -2))
                    if ref >= 3:
                        dve.wait_ge(s_veB, v.lin(1, -2))
                    apart(dve)
                    for tt in range(2):
                        dve.bn_aggr(mvb[:, tt, :], stb[:, tt, :]).then_inc(s_mvB, 1)
                if post:
                    dve.wait_ge(s_y, v.lin(1))
                    apart(dve)
                    for tt in range(2):
                        dve.bn_stats(st[:, tt, :], halfw(y, tt)).then_inc(s_stA, 1)
                if has(ref, 3, PAIRS):
                    for m in range(H):
                        dve.wait_ge(s_hi, v.lin(2, -6 + H))
                        dve.tensor_tensor(ring(lo, v, ref, 3, m), tposed(m), ring(hi, v, ref, 3, m).bitcast(f32),
                                          ALU.subtract).then_inc(s_lo, 1)
                if post:
                    dve.wait_ge(s_stA, v.lin(2))
                    apart(dve)
                    for tt in range(2):
                        dve.bn_aggr(mv[:, tt, :], st[:, tt, :]).then_inc(s_mvA, 1)
                    dve.wait_ge(s_mvA, v.lin(2))
                    for tt in range(2):
                        dve.scalar_tensor_tensor(halfw(y, tt), halfw(y, tt), mv[:, tt, 0:1], gag[:, :],
                                                 ALU.subtract, ALU.mult).then_inc(s_tmpA, 1)
                if rec:
                    adds(s_r, s_pre, v, 1, 0, v.lin(1), ref < G0)
                    if ref == SP0 - 1:
                        dve.wait_ge(s_tanh, 4 * SP0)
                        dve.tensor_copy(h_skip[:, :].rearrange("p (m n) -> p m n", m=H), hs[:, 1, :, :]).then_inc(s_skip, 1)
                if has(ref, 2, PAIRS):
                    if ref >= 3:
                        dve.wait_ge(s_T, v.lin(1, -2))
                    for tt in range(2):
                        dve.wait_ge(s_mvB, v.lin(2, tt - 3))
                        dve.scalar_tensor_tensor(halfw(h2tok, tt), row(v.lin(1, -2), 1, tt * D, D), mvb[:, tt, 0:1],
                                                 cb1[:, :], ALU.subtract, ALU.mult).then_inc(s_tmpB, 1)
                if post:
                    dve.wait_ge(s_rA, v.lin(1))
                    dve.wait_ge(s_xg, v.lin(1))
                    for tt in range(2):
                        dve.wait_ge(s_tmpA, v.lin(2, -1 + tt))
                        dve.scalar_tensor_tensor(row(v.lin(1, -1), 1, tt * D, D), halfw(y, tt), rstd[:, tt:tt + 1],
                                                 halfw(xin[:, bk, :], tt), ALU.mult, ALU.add).then_inc(s_x1, 1)
                if post:
                    for tt in range(2):
                        dve.wait_ge(s_x1, v.lin(2, tt - 1))
                        apart(dve)
                        dve.bn_stats(stb[:, tt, :], row(v.lin(1, -1), 1, tt * D, D)).then_inc(s_stB, 1)
                if outp:
                    dve.wait_ge(s_W, v.lin(1, -O0 + 1))
                    if pos(ref) == 0:
                        dve.wait_ge(s_u, 2 * ((ref - O0) // GROUP + 1))
                    if ref > O0:
                        dve.wait_ge(s_TO, v.lin(1, -O0 if ref < TAIL else -O0 - 1))
                    p = v.lin(1, -O0 - GROUP * ((ref - O0) // GROUP))
                    for m in range(H):
                        dve.tensor_tensor(
                            ow_of(ref)[:, m * GC:(m + 1) * GC].rearrange("p (t b k) -> p b t k", t=2, b=NB),
                            psW_of(ref)[:, m * GC:(m + 1) * GC].rearrange("p (b t k) -> p b t k", b=NB, t=2),
                            uvec[:, m:m + 1, bass.ds(p * (2 * K), 2 * K)].rearrange("p o (t k) -> p o t k", t=2)
                            .broadcast_to([P, NB, 2, K]),
                            ALU.add).then_inc(s_ws, 1)
                if has(ref, O0 + 1, PAIRS):
                    dve.wait_ge(s_TO, v.lin(1, -O0))
                    x1 = row(v.lin(1, -O0 - 1), 1)
                    dve.tensor_tensor(x1, psO_of(ref - 1)[:, :], x1, ALU.add).then_inc(s_fin, 1)
                if has(ref, G0, PAIRS):
                    dve.wait_ge(s_f, v.lin(2, -2 * G0 + 2))
                    if pos(ref) == 0:
                        prev = c0[:, :].rearrange("p (m o) -> p m o", o=1).broadcast_to([P, H, GC])
                    else:
                        prev = cst[:, :, :]
                    dve.tensor_tensor(gf[:, :, :], gf[:, :, :], prev, ALU.mult).then_inc(s_fc, 1)
                if ref == 1:
                    initial()
                if ref == PAIRS + 1:
                    dve.tensor_tensor(pre[:, :].rearrange("p (m n) -> p m n", m=H), hs[:, 1, :, :],
                                      h_end[:, :].rearrange("p (m n) -> p m n", m=H), ALU.subtract).then_inc(k_diff, 1)
                    dve.wait_ge(k_diff, 1)
                    near = y[:, 0:D]
                    dve.tensor_scalar(near, pre[:, :], -TOL, None, ALU.is_ge).then_inc(k_diff, 1)
                    dve.wait_ge(k_diff, 2)
                    dve.scalar_tensor_tensor(pre[:, :], pre[:, :], TOL, near, ALU.is_le, ALU.mult).then_inc(k_diff, 1)
                    dve.wait_ge(k_diff, 3)
                    dve.reduce_sum(cnt[:, :], pre[:, :], AX.X).then_inc(k_diff, 1)
                if ref == TAIL - 1:
                    dve.wait_ge(k_sum, 1)
                    dve.tensor_scalar(miss[:, :], psR[0:1, 0:1], P * D - 0.5, float(K), ALU.is_lt, ALU.mult).then_inc(k_diff, 1)
                    dve.wait_ge(k_diff, 5)
                    dve.tensor_copy(again[:, :], miss[:, :]).then_inc(k_flag, 1)

            def body():
                n_tab[0] = 0
                prepare()
                dve.tensor_copy(hs[:, 1, :, :], h_skip[:, :].rearrange("p (m n) -> p m n", m=H)).then_inc(a_end, 1)
                walk(dve, RUNS1, unit1)
                dve.wait_ge(a_tanh, 4 * RP1)
                dve.tensor_copy(h_end[:, :].rearrange("p (m n) -> p m n", m=H), hs[:, 1, :, :]).then_inc(a_end, 1)
                dve.wait_ge(a_end, 2)
                to = hs[:, 1, :, :].rearrange("p m (b k) -> p (m b) k", b=NB)
                dve.tensor_copy(to[:, :, 1:K], h_end[:, :].rearrange("p (m k) -> p m k", k=K)[:, :, 0:K - 1]).then_inc(a_end, 1)
                dve.memset(to[:, :, 0:1], 0.0).then_inc(a_end, 1)
                dve.wait_ge(a_xb, PAIRS)
                walk(dve, RUNS2, unit2)

            rounds(dve, body, "dve")

        @block.tensor
        def _(pe):
            pe.wait_ge(q_ident, 6)
            def table(j, ps):
                pe.wait_ge(q_wm[j], 16)
                for k in range(H):
                    last = pe.matmul(ps[:, :], scE[:, k, :, :].rearrange("p b n -> p (b n)"), wm[j][:, k, :],
                                     start=(k == 0), stop=(k == H - 1))
                last.then_inc(q_mod, 1)

            def weight(name):
                pe.wait_ge(q_w[name], 16)
                n, last, split = place(name)
                if last is None and BANK[name] is psO:
                    pe.wait_ge(q_tab, 14)
                if last is not None:
                    pe.wait_ge(q_whi, last + 1)
                    if split:
                        pe.wait_ge(q_wcopy, split)
                for k in range(H):
                    for m in range(H):
                        ins = pe.transpose(BANK[name][:, k * D + m * P:k * D + (m + 1) * P],
                                           raw[name][:, m, k * P:(k + 1) * P], ident[:, :])
                ins.then_inc(q_wT, 1)

            def prepare():
                pe.wait_ge(q_silu, 1)
                for k in range(H):
                    last = pe.transpose(psR[:, k * NB:(k + 1) * NB], csig[:, k * P:(k + 1) * P], ident[0:NB, 0:NB])
                last.then_inc(q_scTp, 1)
                pe.wait_ge(q_scT, 2)
                table(0, psC)
                weight("B")
                weight("A")

            def tables():
                table(1, psO)
                table(2, psF)
                for m in range(H):
                    for k in range(H):
                        last = pe.matmul(psR[:, D + m * NB:D + (m + 1) * NB], wm[2][:, k, D + m * P:D + (m + 1) * P],
                                         scT[:, k, :], start=(k == 0), stop=(k == H - 1))
                last.then_inc(q_mod, 1)

            def recur(sem_in, sem_free, sem_out, v, tt, back, first, apart):
                for k in range(H):
                    if not first:
                        pe.wait_ge(sem_in, v.lin(4, -4 * back + 2 * tt - 1 + k))
                    for m in range(H):
                        if k == 0 and m == 1 and apart and not first:
                            pe.wait_ge(sem_free, v.lin(4, -4 * back + 2 * tt))
                        ps = (psR, psF)[m][:, 0:P] if apart else psR[:, m * P:(m + 1) * P]
                        ins = pe.matmul(ps, AT[:, k, m * P:(m + 1) * P], hs[:, 1 - tt, k, :],
                                        start=(k == 0 and (apart or m == 0)), stop=(k == H - 1 and (apart or m == H - 1)),
                                        skip_group_check=True)
                        if k == H - 1 and apart:
                            ins.then_inc(sem_out, 1)
                if not apart:
                    ins.then_inc(sem_out, H)

            def unit1(v, ref):
                rec = has(ref, R1LAG, RP1)
                if rec:
                    if ref == R1LAG:
                        pe.wait_ge(a_end, 1)
                        pe.wait_ge(q_whi, 2)
                    recur(a_tanh, a_pre, a_r, v, 0, R1LAG, ref == R1LAG, True)
                def times_b(back, first, end):
                    if not has(ref, back, PAIRS):
                        return
                    if first == 0:
                        if ref == back:
                            pe.wait_ge(q_whi, 1)
                            pe.wait_ge(q_wlo, 1)
                        else:
                            pe.wait_ge(a_xb, v.lin(1, -back))
                        pe.wait_ge(a_hT, v.lin(1, 1 - back))
                        pe.wait_ge(a_hl, v.lin(1, 1 - back))
                    for n in range(first, end):
                        m, k = n // (3 * H), n // 3 % H
                        w, h = ((whi, hmT_hi), (whi, hmT_lo), (wlo, hmT_hi))[n % 3]
                        last = pe.matmul(psB[:, m * 2 * P:(m + 1) * 2 * P], w["B"][:, k, m * P:(m + 1) * P],
                                         h[:, (ref - back) % 2, k * 2 * P:(k + 1) * 2 * P],
                                         start=(n % (3 * H) == 0), stop=(n % (3 * H) == 3 * H - 1))
                    if end == 3 * H * H:
                        last.then_inc(a_B, 1)

                times_b(4, 0, 8)
                if rec:
                    recur(a_tanh, a_pre, a_r, v, 1, R1LAG, False, True)
                times_b(4, 8, 3 * H * H)
                if has(ref, 2, PAIRS):
                    if ref >= 4:
                        pe.wait_ge(a_hT, v.lin(1, -3))
                        pe.wait_ge(a_hl, v.lin(1, -3))
                    for tt in range(2):
                        pe.wait_ge(a_h, v.lin(2, tt - 3))
                        for m in range(H):
                            last = pe.transpose((psT, psC)[ref % 2][:, m * 2 * P + tt * P:m * 2 * P + (tt + 1) * P],
                                                htok[:, ref % 2, tt * D + m * P:tt * D + (m + 1) * P], ident[:, :])
                    last.then_inc(a_T, 1)
                if ref == 0:
                    tables()
                if ref == 1:
                    weight("C")

            def split3(ps, name, xhi, xlo, start, stop):
                n = 0
                for m in range(H):
                    for k in range(H):
                        for w, xx in ((whi, xhi), (whi, xlo), (wlo, xhi)):
                            n += 1
                            last = pe.matmul(ps[:, m * GC:(m + 1) * GC], w[name][:, k, m * P:(m + 1) * P], xx(k),
                                             start=(start and n == 1), stop=(stop and n == 6 * H), skip_group_check=True)
                return last

            def unit2(v, ref):
                rec, gates = has(ref, 0, PAIRS), has(ref, G0, PAIRS)
                g, b = grp(ref), v.lin(1, -G0 - GROUP * grp(ref))

                def project(tt, back):
                    if ref - back < CS:
                        pe.wait_ge(s_tanh, v.lin(4, -4 * back + 2 * tt + 2))
                        for k in range(H):
                            last = pe.matmul(psC[:, tt * D:(tt + 1) * D], hs[:, tt, k, :], whole("C")[:, k, :],
                                             start=(k == 0), stop=(k == H - 1))
                        return last
                    pe.wait_ge(s_hsh, v.lin(2, -2 * back - 2 * CS + tt + 1))
                    pe.wait_ge(s_hsl, v.lin(2, -2 * back - 2 * CS + tt + 1))
                    n = 0
                    for k in range(H):
                        for h, c in ((hs_hi, whi), (hs_hi, wlo), (hs_lo, whi)):
                            n += 1
                            last = pe.matmul(psC[:, tt * D:(tt + 1) * D], h[:, tt, k, :], c["C"][:, k, :],
                                             start=(n == 1), stop=(n == 3 * H))
                    return last

                def gate_x(n):
                    if not gates:
                        return
                    if n == 0 and pos(ref) == 0:
                        pe.wait_ge(s_hi, 2 * GROUP * (g + 1))
                        pe.wait_ge(s_lo, 2 * GROUP * (g + 1))
                    if ref > G0:
                        pe.wait_ge((s_f, s_i, s_g)[n], v.lin(2, -2 * G0))
                    split3((psF, psI, psG)[n], ("wf", "wi", "wc")[n],
                           lambda k: hi[:, g % 2, k, bass.ds(b, 1), :].rearrange("p o n -> p (o n)"),
                           lambda k: lo[:, g % 2, k, bass.ds(b, 1), :].rearrange("p o n -> p (o n)"), True, False)

                def gate_c(n):
                    if not gates:
                        return
                    if pos(ref) == 0:
                        xhi, xlo = (lambda k: c0hi[:, k:k + 1].broadcast_to([P, GC])), (lambda k: c0lo[:, k:k + 1].broadcast_to([P, GC]))
                    else:
                        xhi, xlo = (lambda k: chi[:, k, :]), (lambda k: clo[:, k, :])
                        if n == 0:
                            pe.wait_ge(s_chi, v.lin(1, -G0 - g))
                            pe.wait_ge(s_clo, v.lin(1, -G0 - g))
                    split3((psF, psI, psG)[n], ("uf", "ui", "uc")[n], xhi, xlo, False, True).then_inc(s_gate, 1)

                if ref == G0:
                    pe.wait_ge(q_whi, len(NAMES))
                    pe.wait_ge(q_wlo, len(whi))
                    pe.wait_ge(q_tables, 1)
                if rec:
                    if ref == 0:
                        pe.wait_ge(a_end, 4)
                    recur(s_tanh, s_pre, s_r, v, 0, 0, ref == 0, ref < G0)
                if has(ref, 1, PAIRS):
                    project(1, 1).then_inc(s_C, 1)
                if has(ref, O0, PAIRS):
                    if ref == TAIL:
                        pe.wait_ge(s_f, 2 * PAIRS)
                    elif ref > O0:
                        pe.wait_ge(s_ws, v.lin(2, -2 * O0 if ref < TAIL else -2 * O0 - 2))
                    og = (ref - O0) // GROUP
                    p = v.lin(1, -O0 - GROUP * og)
                    split3(psW_of(ref), "wo", lambda k: hi[:, og % 2, k, :, bass.ds(p * (2 * K), 2 * K)],
                           lambda k: lo[:, og % 2, k, :, bass.ds(p * (2 * K), 2 * K)], True, True).then_inc(s_W, 1)
                if has(ref, O0 + 1, PAIRS):
                    pe.wait_ge(s_ob, v.lin(2, -2 * O0))
                    if ref == TAIL + 1:
                        pe.wait_ge(s_i, 2 * PAIRS)
                    elif ref > O0 + 1:
                        pe.wait_ge(s_fin, v.lin(1, -O0 - 1 if ref - 1 < TAIL else -O0 - 2))
                    for tt in range(2):
                        for m in range(H):
                            last = pe.transpose(psO_of(ref - 1)[:, tt * D + m * P:tt * D + (m + 1) * P],
                                                ow_of(ref - 1)[:, m * GC + tt * P:m * GC + (tt + 1) * P], ident[:, :])
                    last.then_inc(s_TO, 1)
                gate_x(0)
                if has(ref, 3, PAIRS):
                    pe.wait_ge(s_h2, v.lin(1, -2))
                    if ref > 3:
                        pe.wait_ge(s_hi, v.lin(2, -6))
                        pe.wait_ge(s_lo, v.lin(2, -6))
                    for tt in range(2):
                        for m in range(H):
                            last = pe.transpose(psT[:, m * 2 * P + tt * P:m * 2 * P + (tt + 1) * P],
                                                h2tok[:, tt * D + m * P:tt * D + (m + 1) * P], ident[:, :])
                    last.then_inc(s_T, 1)
                if rec:
                    recur(s_tanh, s_pre, s_r, v, 1, 0, False, ref < G0)
                if ref == PAIRS + 2:
                    pe.wait_ge(k_diff, 4)
                    pe.matmul(psR[0:1, 0:1], cnt[:, :], ones[:, :], start=True, stop=True).then_inc(k_sum, 1)
                if has(ref, O0, PAIRS) and pos(ref) == 0:
                    pe.wait_ge(s_c, ref - G0)
                    pe.wait_ge(s_y, min(ref, PAIRS))
                    for m in range(H):
                        for k in range(H):
                            last = pe.matmul(psC[:, m * GC:(m + 1) * GC], uoT[:, k, m * P:(m + 1) * P], cst[:, k, :],
                                             start=(k == 0), stop=(k == H - 1))
                    last.then_inc(s_U, 1)
                gate_x(1)
                gate_x(2)
                if rec:
                    if ref >= 1:
                        pe.wait_ge(s_y, v.lin(1))
                    if has(ref, O0, PAIRS) and pos(ref) == 0:
                        pe.wait_ge(s_u, 2 * ((ref - O0) // GROUP + 1))
                    project(0, 0)
                if ref < len(LATE):
                    weight(LATE[ref])
                gate_c(0)
                gate_c(1)
                gate_c(2)

            def body():
                prepare()
                walk(pe, RUNS1, unit1)
                pe.wait_ge(q_whi, len(EARLY))
                pe.wait_ge(q_wlo, 2)
                walk(pe, RUNS2, unit2)

            rounds(pe, body, "pe")


_INS = ["L0_attn_x", "L0_attn_A", "L0_attn_B", "L0_attn_C", "L0_attn_gamma", "L0_attn_beta",
        "L0_ffn_wf", "L0_ffn_uf", "L0_ffn_bf", "L0_ffn_wi", "L0_ffn_ui", "L0_ffn_bi", "L0_ffn_wc", "L0_ffn_uc",
        "L0_ffn_bc", "L0_ffn_wo", "L0_ffn_uo", "L0_ffn_bo", "L0_ffn_in_c", "L0_c", "L0_wmod"]


def kernel(**inputs):
    import numpy as _np
    import concourse.bacc as _bacc
    from concourse import mybir as _mybir
    from concourse.bass_utils import run_bass_kernel_spmd as _run

    nc = _bacc.Bacc("TRN2", target_bir_lowering=False, num_devices=1)
    arrays, args = {}, []
    for name in _INS:
        a = _np.ascontiguousarray(inputs[name])
        arrays[f"in_{name}_dram"] = a
        args.append(nc.dram_tensor(f"in_{name}_dram", a.shape, _mybir.dt.from_np(a.dtype), kind="ExternalInput").ap())
    shape = inputs["L0_attn_x"].shape
    args.append(nc.dram_tensor("out_0_dram", shape, _mybir.dt.float32, kind="ExternalOutput").ap())
    adaln_kernel(nc, *args)
    r = _run(nc, [arrays], core_ids=[0])
    return r.results[0]["out_0_dram"]
```

```python
import concourse.bass as bass
from concourse import mybir
from contextlib import ExitStack



class At:

    def __init__(self, i, c):
        self.i, self.c = i, c

    def lin(self, k, c0=0):
        c = k * self.c + c0
        return c if isinstance(self.i, int) else self.i * (2 * k) + c

    def half(self, k, back, c0=0):
        c = k * ((self.c - back) // 2) + c0
        return c if isinstance(self.i, int) else self.i * k + c


def adaln_kernel(nc, x, A, B, C, gamma, beta, wf, uf, bf, wi, ui, bi, wc, uc, bc, wo, uo, bo, in_c, cond, wmod, out):
    f32 = mybir.dt.float32
    f32r = mybir.dt.float32r
    i32 = mybir.dt.int32
    ALU = mybir.AluOpType
    ACT = mybir.ActivationFunctionType
    AX = mybir.AxisListType

    P = 128
    NB, S, D = x.shape
    K = P // NB
    L = S // K
    H = D // P
    SKIP = 8
    PAIRS = L // 2
    SP0 = SKIP // 2
    RP1 = PAIRS - SP0
    W = 2 * D
    GROUP = 8
    NG = PAIRS // GROUP
    GC = 2 * GROUP * K
    EPS = 1e-5
    TOL = 2.0 ** -18

    G0 = GROUP + 3
    O0 = G0 + GROUP
    UNITS2 = O0 + PAIRS + 2
    TAIL = G0 + PAIRS
    CS = G0 - 1
    C0W = 8
    R1LAG = 6
    UNITS1 = PAIRS + 4
    LATE = ["wf", "wi", "wc", "uf", "ui", "uc", "wo", "uo"]
    LOADS = {1: ["B", "A", "wmod", "C"], 2: ["affine"], 3: ["wf"], 4: ["wi"], 5: ["wc"], 6: ["bias"]}
    RAW = 8

    x_v = x.rearrange("b (k t) d -> (b k) (t d)", k=K)
    out_v = out.rearrange("b (k t) d -> (b k) (t d)", k=K)
    wmod_v = wmod.rearrange("(k p) n -> p k n", p=P)
    h_park = nc.dram_tensor("h_park", [PAIRS, P, W], f32, kind="Internal").ap()

    ctx = ExitStack()
    with ctx:
        def sb(name, shape, dt=f32):
            return ctx.enter_context(nc.sbuf_tensor(name, shape, dt))

        def sem(name):
            return ctx.enter_context(nc.semaphore(name))

        ident = sb("ident", [P, P])
        ones = sb("ones", [P, 1])
        mhalf = sb("mhalf", [P, 2])
        epst = sb("epst", [P, 2])
        AT = sb("AT", [P, H, D])
        uoT = sb("uoT", [P, H, D])
        SPLIT = ["C", "wf", "wi", "wc", "uf", "ui", "uc", "wo"]
        whi = {n: sb(n + "T_hi", [P, H, D], f32r) for n in SPLIT}
        wlo = {n: sb(n + "T_lo", [P, H, D], f32r) for n in SPLIT}
        gag = sb("gag", [P, D])
        gab = sb("gab", [P, D])
        cb1 = sb("cb1", [P, D])
        sbt = sb("sbt", [P, D])
        gbT = sb("gbT", [P, H, NB])
        bias = sb("bias", [P, 4, H])
        bias0 = sb("bias0", [P, 3, H])
        c0 = sb("c0", [P, H])
        c0hi = sb("c0hi", [P, H], f32r)
        c0lo = sb("c0lo", [P, H], f32r)

        state = sb("state", [P, PAIRS * W])
        hi = sb("hi", [P, 2, H, NB, GC], f32r)
        lo = sb("lo", [P, 2, H, NB, GC], f32r)
        xin = sb("xin", [P, 2, W])
        htok = sb("htok", [P, 2, W])
        h2tok = sb("h2tok", [P, W])
        y = sb("y", [P, W])[:, :]
        ow = sb("ow", [P, W])[:, :]
        pre = sb("pre", [P, D])
        hs = sb("hs", [P, 2, H, P])
        hs_hi = sb("hs_hi", [P, 2, H, P], f32r)
        hs_lo = sb("hs_lo", [P, 2, H, P], f32r)
        h_skip = sb("h_skip", [P, D])
        h_end = sb("h_end", [P, D])
        gf = sb("gf", [P, H, GC])
        gi = sb("gi", [P, H, GC])
        gg = sb("gg", [P, H, GC])
        cst = sb("cst", [P, H, GC])
        chi = sb("chi", [P, H, GC], f32r)
        clo = sb("clo", [P, H, GC], f32r)
        uvec = sb("uvec", [P, H, GC])
        whi["B"], wlo["B"] = chi, clo
        ca1, sa = uvec[:, 0, :], uvec[:, 1, :]
        hmT_hi, hmT_lo = (r[:, 0, 0, 0:4, :].rearrange("p (i c) n -> p i (c n)", i=2) for r in (hi, lo))
        st = sb("st", [P, 2, 6])
        stb = sb("stb", [P, 2, 6])
        mv = sb("mv", [P, 2, 2])
        mvb = sb("mvb", [P, 2, 2])
        ve = sb("ve", [P, 2])
        rstd = sb("rstd", [P, 2])
        rstdb = sb("rstdb", [P, 2])
        cnt = sb("cnt", [P, 1])
        miss = sb("miss", [1, 1])
        again = sb("again", [1, 1], i32)

        EARLY = ["B", "A", "C"]
        NAMES = EARLY + LATE
        at = RAW * W
        raw = {n: state[:, at + i * W:at + (i + 1) * W].rearrange("p (m d) -> p m d", m=H) for i, n in enumerate(EARLY)}
        at += len(EARLY) * W
        for i, n in enumerate(LATE):
            raw[n] = (gf, gi, gg)[i % 3][:, :, :]
        wm = [state[:, at + 2 * j * W:at + 2 * (j + 1) * W].rearrange("p (k n) -> p k n", k=H) for j in range(3)]
        at += 6 * W
        gamma_b = state[:, at:at + D]
        beta_b = state[:, at + D:at + 2 * D]
        cn = state[0:NB, at + W:at + W + D]
        csig = state[0:NB, at + W + D:at + 2 * W]
        at += 2 * W
        scT = state[:, at:at + H * NB].rearrange("p (k b) -> p k b", k=H)
        scE = state[:, at + D:at + D + H * P].rearrange("p (k b n) -> p k b n", k=H, b=NB)
        at += W
        ga = state[:, at:at + D]
        gmag = state[:, at + D:at + 2 * D]
        gs = state[:, at + 2 * D:at + 2 * D + H * NB].rearrange("p (k b) -> p k b", k=H)
        gm = state[:, at + 3 * D:at + 3 * D + H * NB].rearrange("p (k b) -> p k b", k=H)

        def bank(name):
            return ctx.enter_context(nc.psum_tensor(name, [P, 512], f32))

        psR, psC, psT, psF, psI, psG, psW, psO = (bank(n) for n in (
            "psR", "psC", "psT", "psF", "psI", "psG", "psW", "psO"))
        BANK = dict(zip(NAMES, (psI, psG, psI, psG, psO, psI, psG, psO, psI, psG, psO)))

        def place(name):
            before = [i for i in range(NAMES.index(name)) if BANK[NAMES[i]] is BANK[name]]
            last = before[-1] if before else None
            return last, sum(n in whi for n in NAMES[:last + 1]) if before else 0

        def nth_split(name):
            return sum(n in whi for n in NAMES[:NAMES.index(name)])

        def whole(name):
            if name == "B":
                return state[:, 0:W].rearrange("p (k d) -> p k d", k=H)
            if name == "C":
                return ow.rearrange("p (k d) -> p k d", k=H)
            return (cst, uvec)[LATE.index(name) % 2][:, :, :]

        def ow_of(u):
            return ow if u < TAIL else (y, h2tok[:, :], ow)[(u - TAIL) % 3]

        def psW_of(u):
            return psW if u < TAIL else (psF, psG, psW)[(u - TAIL) % 3]

        def psO_of(u):
            return psO if u < TAIL else (psI, psO)[(u - TAIL) % 2]

        def back_of(u):
            back = 1 if u <= TAIL else 2
            return back if has(u, O0 + back, PAIRS) and u != TAIL + 1 else None

        q_ident = sem("q_ident")
        q_table = sem("q_table")
        q_w = {n: sem("q_w_" + n) for n in NAMES}
        q_wm = [sem(f"q_wm{j}") for j in range(3)]
        q_cond = sem("q_cond")
        q_affine = sem("q_affine")
        q_bias = sem("q_bias")
        q_wT = sem("q_wT")
        q_whi = sem("q_whi")
        q_wcopy = sem("q_wcopy")
        q_wlo = sem("q_wlo")
        q_sig = sem("q_sig")
        q_silu = sem("q_silu")
        q_scTp = sem("q_scTp")
        q_scT = sem("q_scT")
        q_mod = sem("q_mod")
        q_tab = sem("q_tab")
        q_tables = sem("q_tables")
        q_uc0 = sem("q_uc0")
        q_bias0 = sem("q_bias0")
        a_x = [sem(f"a_xin{i}") for i in range(2)]
        a_stats = sem("a_stats")
        a_mv = sem("a_mv")
        a_ve = sem("a_ve")
        a_rstd = sem("a_rstd")
        a_tmp = sem("a_tmp")
        a_h = sem("a_h")
        a_park = [sem(f"a_park{i}") for i in range(2)]
        a_T = sem("a_T")
        a_hT = sem("a_hT")
        a_hl = sem("a_hl")
        a_sc = sem("a_sc")
        a_B = sem("a_B")
        a_xb = sem("a_xb")
        a_r = sem("a_r")
        a_pre = sem("a_pre")
        a_tanh = sem("a_tanh")
        a_end = sem("a_end")
        s_x = [sem(f"s_xin{i}") for i in range(2)]
        s_h = [sem(f"s_hin{i}") for i in range(2)]
        s_r = sem("s_r")
        s_pre = sem("s_pre")
        s_tanh = sem("s_tanh")
        s_hsh = sem("s_hsh")
        s_hsl = sem("s_hsl")
        s_skip = sem("s_skip")
        s_C = sem("s_C")
        s_y = sem("s_y")
        s_stA = sem("s_stA")
        s_mvA = sem("s_mvA")
        s_veA = sem("s_veA")
        s_rA = sem("s_rA")
        s_tmpA = sem("s_tmpA")
        s_xg = sem("s_xg")
        s_x1 = sem("s_x1")
        s_stB = sem("s_stB")
        s_mvB = sem("s_mvB")
        s_veB = sem("s_veB")
        s_rB = sem("s_rB")
        s_tmpB = sem("s_tmpB")
        s_scB = sem("s_scB")
        s_h2 = sem("s_h2")
        s_T = sem("s_T")
        s_hi = sem("s_hi")
        s_lo = sem("s_lo")
        s_gate = sem("s_gate")
        s_f = sem("s_f")
        s_i = sem("s_i")
        s_g = sem("s_g")
        s_fc = sem("s_fc")
        s_ig = sem("s_ig")
        s_c = sem("s_c")
        s_chi = sem("s_chi")
        s_clo = sem("s_clo")
        s_U = sem("s_U")
        s_u = sem("s_u")
        s_W = sem("s_W")
        s_ws = sem("s_ws")
        s_ot = sem("s_ot")
        s_ob = sem("s_ob")
        s_TO = sem("s_TO")
        s_fin = sem("s_fin")
        s_out = sem("s_out")
        k_diff = sem("k_diff")
        k_sum = sem("k_sum")
        k_flag = sem("k_flag")
        s_apart = sem("s_apart")
        of_start = [*q_w.values(), *q_wm, q_cond, q_affine, q_bias, q_wT, q_whi, q_wcopy, q_wlo, q_sig, q_silu, q_scTp,
                    q_scT, q_mod, q_tab, q_tables, q_uc0, q_bias0, *a_x, a_stats, a_mv, a_ve, a_rstd, a_tmp, a_h, *a_park, a_T, a_hT,
                    a_hl, a_sc, a_B, a_xb, a_r, a_pre, a_tanh, a_end]
        of_middle = [*s_x, *s_h, s_r, s_pre, s_tanh, s_hsh, s_hsl, s_skip, s_C, s_y, s_stA, s_mvA, s_veA, s_rA, s_tmpA,
                     s_xg, s_x1, s_stB, s_mvB, s_veB, s_rB, s_tmpB, s_scB, s_h2, s_T, s_hi, s_lo, s_gate, s_f, s_i, s_g,
                     s_fc, s_ig, s_c, s_chi, s_clo, k_diff, k_sum]
        of_end = [s_U, s_u, s_W, s_ws, s_ot, s_ob, s_TO, s_fin, s_out, k_flag, s_apart]
        r_over = sem("r_over")
        r_next = sem("r_next")

        def ranges(cuts, end):
            return list(zip(cuts, cuts[1:] + [end]))

        RUNS1 = ranges([*range(max(LOADS) + 2), RP1, RP1 + 1, RP1 + 2, RP1 + 3, RP1 + 4, RP1 + 5, RP1 + 6], UNITS1)
        cuts = {*range(G0 + 1), PAIRS, PAIRS + 1, PAIRS + 2, PAIRS + 3, O0 + 1, O0 + 2, *range(TAIL, UNITS2)}
        for g in range(NG + 1):
            cuts |= {G0 + GROUP * g, G0 + GROUP * g + 1, G0 + GROUP * g - 1}
        RUNS2 = ranges(sorted(c for c in cuts if c < UNITS2), UNITS2)

        def walk(eng, runs, unit):
            for a, b in runs:
                n = (b - a) // 2
                if n < 2:
                    n = 0
                if n:
                    with eng.Fori(0, n) as i:
                        unit(At(i, a), a)
                        unit(At(i, a + 1), a + 1)
                for c in range(a + 2 * n, b):
                    unit(At(0, c), c)

        def pair1(v, ref, back):
            return v.lin(1, SP0 - back) if ref - back < RP1 else v.lin(1, -RP1 - back)

        def has(ref, first, n):
            return first <= ref < first + n

        def grp(ref):
            return (ref - G0) // GROUP

        def pos(ref):
            return (ref - G0) % GROUP

        def row(p, off=0, n=W):
            return state[:, bass.ds(p * W + off, n)]

        def tposed(m):
            return psT[:, m * 2 * P:(m + 1) * 2 * P].rearrange("p (t b k) -> p t b k", t=2, b=NB)

        def ring(buf, v, ref, back, m):
            g, p = (ref - back) // GROUP, v.lin(1, -back - GROUP * ((ref - back) // GROUP))
            part = buf[:, g % 2, m, :, bass.ds(p * (2 * K), 2 * K)]
            return part.rearrange("p b (t k) -> p t b k", t=2)

        def apart(eng):
            eng.sem_inc(s_apart, 1)

        def rounds(eng, body, name):
            left = eng.alloc_register("rounds_" + name)
            eng.reg_mov(left, K)
            with eng.Fori(0, left) as r:
                body()
                eng.wait_ge(k_flag, 1)
                eng.reg_mov(left, eng.value_load(again[0:1, 0:1], min_val=0, max_val=K))
                eng.drain().then_inc(r_over, 1)
                eng.wait_ge(r_next, r + 1)

        block = ctx.enter_context(nc.Block())

        @block.sync
        def _(sp):
            weights = dict(zip(("A", "B", "C", "wf", "wi", "wc", "uf", "ui", "uc", "wo", "uo"),
                               (A, B, C, wf, wi, wc, uf, ui, uc, wo, uo)))

            def load(what):
                if what == "wmod":
                    for j in (1, 2):
                        sp.dma_start(wm[j], wmod_v[:, :, j * W:(j + 1) * W]).then_inc(q_wm[j], 16)
                elif what == "affine":
                    for dst, src in ((gamma_b, gamma), (beta_b, beta)):
                        sp.dma_start(dst, src.rearrange("(o n) -> o n", o=1).broadcast_to([P, D])).then_inc(q_affine, 16)
                elif what == "bias":
                    for j, src in enumerate((bf, bi, bc, bo)):
                        sp.dma_start(bias[:, j, :], src.rearrange("(m p) -> p m", p=P),
                                     allow_slow_non_contiguous=True).then_inc(q_bias, 16)
                    sp.dma_start(c0[:, :], in_c.rearrange("(m p) -> p m", p=P),
                                 allow_slow_non_contiguous=True).then_inc(q_bias, 16)
                else:
                    sp.dma_start(raw[what], weights[what].rearrange("(m p) d -> p m d", p=P)).then_inc(q_w[what], 16)

            def unit1(v, ref):
                if has(ref, 0, PAIRS):
                    if ref >= 2:
                        sp.wait_ge(a_tmp, v.lin(2, -2))
                    p = pair1(v, ref, 0)
                    sp.dma_start(xin[:, ref % 2, :], x_v[:, bass.ds(p * W, W)]).then_inc(a_x[ref % 2], 16)
                if has(ref, 2, PAIRS):
                    sp.wait_ge(a_h, v.lin(2, -2))
                    p = pair1(v, ref, 2)
                    sp.dma_start(h_park[bass.ds(p, 1), :, :].rearrange("o p w -> p (o w)"),
                                 htok[:, ref % 2, :]).then_inc(a_park[ref % 2], 16)
                for what in LOADS.get(ref, []):
                    load(what)

            def clear(sems):
                for s in sems:
                    sp.sem_clear(s)

            def unit2(v, ref):
                if has(ref, 0, PAIRS):
                    if ref >= 2:
                        sp.wait_ge(s_x1, v.lin(2, -2))
                    sp.dma_start(xin[:, ref % 2, :], x_v[:, bass.ds(v.lin(W), W)]).then_inc(s_x[ref % 2], 16)
                    sp.dma_start(htok[:, ref % 2, :],
                                 h_park[bass.ds(v.lin(1), 1), :, :].rearrange("o p w -> p (o w)")).then_inc(s_h[ref % 2], 16)
                if 1 <= ref < len(LATE) - 2:
                    sp.wait_ge(q_wT, len(EARLY) + ref)
                    load(LATE[ref + 2])
                back = back_of(ref)
                if back:
                    sp.wait_ge(s_fin, v.lin(1, 1 - O0 - back))
                    sp.dma_start(out_v[:, bass.ds(v.lin(W, -(O0 + back) * W), W)],
                                 row(v.lin(1, -O0 - back))).then_inc(s_out, 16)
                if ref == TAIL:
                    clear(of_start)
                if ref == TAIL + 4:
                    clear(of_middle)

            left = sp.alloc_register("rounds_sp")
            sp.reg_mov(left, K)
            with sp.Fori(0, left) as r:
                sp.dma_start(cn, cond).then_inc(q_cond, 16)
                sp.dma_start(wm[0], wmod_v[:, :, 0:W]).then_inc(q_wm[0], 16)
                walk(sp, RUNS1, unit1)
                sp.wait_ge(a_park[0], 16 * (PAIRS // 2))
                sp.wait_ge(a_park[1], 16 * (PAIRS // 2))
                sp.wait_ge(a_T, PAIRS)
                walk(sp, RUNS2, unit2)
                sp.wait_ge(s_out, 16 * PAIRS)
                sp.wait_ge(k_flag, 1)
                sp.reg_mov(left, sp.value_load(again[0:1, 0:1], min_val=0, max_val=K))
                sp.wait_ge(r_over, r * 4 + 4)
                apart(sp)
                clear(of_end)
                sp.sem_inc(r_next, 1)

        @block.gpsimd
        def _(pool):
            pool.memset(ident[:, :], 0.0).then_inc(q_ident, 1)
            pool.wait_ge(q_ident, 1)
            pool.affine_select(out=ident[:, :], in_=ident[:, :], compare_op=ALU.not_equal, fill=1.0, base=0,
                               pattern=[[-1, P]], channel_multiplier=1).then_inc(q_ident, 1)
            pool.memset(mhalf[:, :], -0.5).then_inc(q_ident, 1)
            pool.memset(ones[:, :], 1.0).then_inc(q_ident, 1)
            pool.memset(epst[:, :], EPS).then_inc(q_ident, 1)
            pool.memset(h_skip[:, :], 0.0).then_inc(q_ident, 1)
            pool.wait_ge(q_ident, 6)

            def weight(name):
                if name in whi:
                    pool.wait_ge(q_wcopy, nth_split(name) + 1)
                    pool.wait_ge(q_whi, NAMES.index(name) + 1)
                    pool.tensor_tensor(wlo[name][:, :, :], whole(name), whi[name][:, :, :].bitcast(f32),
                                       ALU.subtract).then_inc(q_wlo, 1)

            def unit1(v, ref):
                if has(ref, 1, PAIRS):
                    pool.wait_ge(a_mv, v.lin(2))
                    pool.tensor_tensor(ve[:, :], mv[:, :, 1], epst[:, :], ALU.add).then_inc(a_ve, 1)
                    pool.wait_ge(a_ve, v.lin(1))
                    pool.tensor_tensor(rstd[:, :], ve[:, :], mhalf[:, :], ALU.pow).then_inc(a_rstd, 1)
                    if ref == 1:
                        pool.wait_ge(q_tab, 2)
                    for tt in range(2):
                        pool.wait_ge(a_sc, v.lin(2, tt - 1))
                        h = htok[:, (ref - 1) % 2, tt * D:(tt + 1) * D]
                        pool.tensor_tensor(h, h, sa, ALU.add).then_inc(a_h, 1)
                if ref in (1, 4):
                    weight({1: "B", 4: "C"}[ref])

            def state_low(v, tt):
                pool.wait_ge(s_hsh, v.lin(2, -2 * CS + tt + 1))
                pool.tensor_tensor(hs_lo[:, tt, :, :], hs[:, tt, :, :], hs_hi[:, tt, :, :].bitcast(f32),
                                   ALU.subtract).then_inc(s_hsl, 1)

            def unit2(v, ref):
                if has(ref, 3, PAIRS):
                    pool.wait_ge(s_scB, v.lin(2, -4))
                    h2 = h2tok[:, :].rearrange("p (t d) -> p t d", t=2)
                    pool.tensor_tensor(h2, h2, sbt[:, :].rearrange("p (o d) -> p o d", o=1).broadcast_to([P, 2, D]),
                                       ALU.add).then_inc(s_h2, 1)
                if has(ref, G0 + 1, PAIRS):
                    pool.wait_ge(s_i, v.lin(2, -2 * G0))
                    pool.wait_ge(s_g, v.lin(2, -2 * G0))
                    pool.tensor_tensor(gi[:, :, :], gi[:, :, :], gg[:, :, :], ALU.mult).then_inc(s_ig, 1)
                if has(ref, CS, PAIRS - CS):
                    state_low(v, 0)
                if has(ref, 1, PAIRS):
                    pool.wait_ge(s_x[(ref - 1) % 2], v.half(16, 1, 16))
                    xg = xin[:, (ref - 1) % 2, :].rearrange("p (t d) -> p t d", t=2)
                    pool.tensor_tensor(xg, xg, gab[:, :].rearrange("p (o d) -> p o d", o=1).broadcast_to([P, 2, D]),
                                       ALU.add).then_inc(s_xg, 1)
                if has(ref, 2, PAIRS):
                    pool.wait_ge(s_mvB, v.lin(2, -2))
                    if ref >= 3:
                        pool.wait_ge(s_rA, v.lin(1, -1))
                    pool.tensor_tensor(ve[:, :], mvb[:, :, 1], epst[:, :], ALU.add).then_inc(s_veB, 1)
                    pool.wait_ge(s_veB, v.lin(1, -1))
                    pool.tensor_tensor(rstdb[:, :], ve[:, :], mhalf[:, :], ALU.pow).then_inc(s_rB, 1)
                if has(ref, 1, PAIRS):
                    pool.wait_ge(s_mvA, v.lin(2))
                    if ref >= 2:
                        pool.wait_ge(s_rB, v.lin(1, -1))
                    pool.tensor_tensor(ve[:, :], mv[:, :, 1], epst[:, :], ALU.add).then_inc(s_veA, 1)
                    pool.wait_ge(s_veA, v.lin(1))
                    pool.tensor_tensor(rstd[:, :], ve[:, :], mhalf[:, :], ALU.pow).then_inc(s_rA, 1)
                if has(ref, CS, PAIRS - CS):
                    state_low(v, 1)
                if 1 <= ref <= len(LATE):
                    weight(LATE[ref - 1])
                if has(ref, O0, PAIRS):
                    pool.wait_ge(s_ot, v.lin(1, -O0 + 1))
                    for m in range(H):
                        o4 = ow_of(ref)[:, m * GC:(m + 1) * GC].rearrange("p (t b k) -> p t b k", t=2, b=NB)
                        g4 = gbT[:, m:m + 1, :].rearrange("p o (b k) -> p o b k", k=1).broadcast_to([P, 2, NB, K])
                        pool.tensor_tensor(o4, o4, g4, ALU.mult).then_inc(s_ob, 1)

            def body():
                walk(pool, RUNS1, unit1)
                pool.wait_ge(q_tab, 16)
                walk(pool, RUNS2, unit2)

            rounds(pool, body, "pool")

        @block.scalar
        def _(act):
            act.wait_ge(q_ident, 6)
            act.activation(cnt[:, :], ones[:, :], ACT.Sigmoid).then_inc(q_table, 1)
            act.wait_ge(q_table, 1)

            def weight(name):
                act.wait_ge(q_wT, NAMES.index(name) + 1)
                if name in whi:
                    if name in LATE[2:]:
                        act.wait_ge(q_wlo, LATE.index(name) + 1)
                    act.activation(whole(name), BANK[name][:, :].rearrange("p (k d) -> p k d", k=H),
                                   ACT.Copy).then_inc(q_wcopy, 1)
                dst = {"A": AT, "uo": uoT}.get(name)
                dst = whi[name] if dst is None else dst
                act.activation(dst[:, :, :], BANK[name][:, :].rearrange("p (k d) -> p k d", k=H), ACT.Copy).then_inc(q_whi, 1)

            def prepare():
                act.wait_ge(q_cond, 16)
                act.activation(csig, cn, ACT.Sigmoid).then_inc(q_sig, 1)
                weight("B")
                weight("A")

            def tanhs(sem_in, sem_out, v, tt, back, apart):
                if not apart:
                    act.wait_ge(sem_in, v.lin(4, -4 * back + 2 * tt + H))
                    act.activation(hs[:, tt, :, :], pre[:, :].rearrange("p (m n) -> p m n", m=H), ACT.Tanh).then_inc(sem_out, H)
                    return
                for m in range(H):
                    act.wait_ge(sem_in, v.lin(4, -4 * back + 2 * tt + m + 1))
                    act.activation(hs[:, tt, m, :], pre[:, m * P:(m + 1) * P], ACT.Tanh).then_inc(sem_out, 1)

            def unit1(v, ref):
                rec = has(ref, R1LAG, RP1)
                if rec:
                    tanhs(a_pre, a_tanh, v, 0, R1LAG, True)
                if has(ref, 3, PAIRS):
                    act.wait_ge(a_T, v.lin(1, -2))
                    if ref >= 5:
                        act.wait_ge(a_B, v.lin(1, -4))
                    b = (ref - 3) % 2
                    act.activation(hmT_hi[:, b, :], (psT, psC)[b][:, :], ACT.Copy).then_inc(a_hT, 1)
                if rec:
                    tanhs(a_pre, a_tanh, v, 1, R1LAG, True)
                if has(ref, 4, PAIRS):
                    act.wait_ge(a_B, v.lin(1, -3))
                    act.activation(row(pair1(v, ref, 4)), (psW, psO)[ref % 2][:, :], ACT.Copy).then_inc(a_xb, 1)
                if has(ref, 1, PAIRS):
                    act.wait_ge(a_rstd, v.lin(1))
                    for tt in range(2):
                        act.wait_ge(a_tmp, v.lin(2, tt - 1))
                        h = htok[:, (ref - 1) % 2, tt * D:(tt + 1) * D]
                        act.activation(h, h, ACT.Copy, scale=rstd[:, tt:tt + 1]).then_inc(a_sc, 1)
                if ref == 3:
                    weight("C")

            def state_of(v, ref, tt):
                if ref > CS:
                    act.wait_ge(s_hsl, v.lin(2, -2 * CS + tt - 1))
                if ref < G0:
                    for m in range(H):
                        act.wait_ge(s_r, v.lin(4, 2 * tt + m + 1))
                        act.activation(hs[:, tt, m, :], (psR, psF)[m][:, 0:P], ACT.Tanh).then_inc(s_tanh, 1)
                else:
                    tanhs(s_pre, s_tanh, v, tt, G0, False)
                if ref >= CS:
                    act.wait_ge(s_tanh, v.lin(4, 2 * tt + 2))
                    if ref > CS:
                        act.wait_ge(s_C, v.lin(1))
                    act.activation(hs_hi[:, tt, :, :], hs[:, tt, :, :], ACT.Copy).then_inc(s_hsh, 1)

            def unit2(v, ref):
                if 1 <= ref <= len(LATE):
                    weight(LATE[ref - 1])
                if has(ref, 0, PAIRS):
                    state_of(v, ref, 0)
                if has(ref, G0 + 1, PAIRS) and pos(ref - 1) < GROUP - 1:
                    act.wait_ge(s_c, v.lin(1, -G0))
                    act.activation(chi[:, :, :], cst[:, :, :], ACT.Copy).then_inc(s_chi, 1)
                if has(ref, 3, PAIRS):
                    act.wait_ge(s_T, v.lin(1, -2))
                    for m in range(H):
                        act.activation(ring(hi, v, ref, 3, m), tposed(m), ACT.Copy).then_inc(s_hi, 1)
                if has(ref, 0, PAIRS):
                    state_of(v, ref, 1)
                if has(ref, O0, PAIRS) and pos(ref) == 0:
                    act.wait_ge(s_U, (ref - O0) // GROUP + 1)
                    if ref > O0:
                        act.wait_ge(s_ws, 2 * (ref - O0))
                    for m in range(H):
                        act.activation(uvec[:, m, :], psC[:, m * GC:(m + 1) * GC], ACT.Identity,
                                       bias=bias[:, 3, m:m + 1]).then_inc(s_u, 1)
                if has(ref, 2, PAIRS):
                    act.wait_ge(s_rB, v.lin(1, -1))
                    for tt in range(2):
                        act.wait_ge(s_tmpB, v.lin(2, tt - 3))
                        h2 = h2tok[:, tt * D:(tt + 1) * D]
                        act.activation(h2, h2, ACT.Copy, scale=rstdb[:, tt:tt + 1]).then_inc(s_scB, 1)
                if has(ref, O0, PAIRS):
                    act.wait_ge(s_ws, v.lin(2, -2 * O0 + 2))
                    act.activation(ow_of(ref), ow_of(ref), ACT.Tanh).then_inc(s_ot, 1)
                if has(ref, G0, PAIRS):
                    if ref > G0:
                        act.wait_ge(s_c, v.lin(1, -G0))
                    for n, (dst, src, fn, s) in enumerate(((gf, psF, ACT.Sigmoid, s_f), (gi, psI, ACT.Sigmoid, s_i),
                                                           (gg, psG, ACT.Tanh, s_g))):
                        act.wait_ge(s_gate, v.lin(3, -3 * G0 + n + 1))
                        if ref == G0 and n == 0:
                            act.wait_ge(q_bias0, 1)
                        with_bias = bias0 if pos(ref) == 0 else bias
                        for m in range(H):
                            act.activation(dst[:, m, :], src[:, m * GC:(m + 1) * GC], fn,
                                           bias=with_bias[:, n, m:m + 1]).then_inc(s, 1)

            def body():
                prepare()
                walk(act, RUNS1, unit1)
                act.wait_ge(q_bias, 16 * 5)
                walk(act, RUNS2, unit2)

            rounds(act, body, "act")

        @block.vector
        def _(dve):
            dve.wait_ge(q_ident, 6)
            n_tab = [0]

            def halfw(t, tt):
                return t[:, tt * D:(tt + 1) * D]

            def tab(ins):
                n_tab[0] += 1
                ins.then_inc(q_tab, 1)

            def tabs_done():
                dve.wait_ge(q_tab, n_tab[0])

            def prepare():
                dve.wait_ge(q_sig, 1)
                dve.tensor_tensor(csig, cn, csig, ALU.mult).then_inc(q_silu, 1)
                dve.wait_ge(q_scTp, 1)
                dve.tensor_copy(scT, psR[:, 0:H * NB].rearrange("p (k b) -> p k b", k=H)).then_inc(q_scT, 1)
                dve.tensor_copy(scE, psR[:, 0:H * NB].rearrange("p (k b o) -> p k b o", k=H, o=1)
                                .broadcast_to([P, H, NB, K])).then_inc(q_scT, 1)
                dve.wait_ge(a_x[0], 16)
                for tt in range(2):
                    dve.bn_stats(st[:, tt, :], halfw(xin[:, 0, :], tt)).then_inc(a_stats, 1)
                dve.wait_ge(q_mod, 1)
                tab(dve.tensor_scalar(ca1, psC[:, D:W], 1.0, None, ALU.add))
                tab(dve.tensor_copy(sa, psC[:, 0:D]))
                tabs_done()

            def tables():
                dve.wait_ge(q_mod, 4)
                tab(dve.tensor_copy(sbt[:, :], psO[:, D:W]))
                tab(dve.tensor_scalar(cb1[:, :], psF[:, 0:D], 1.0, None, ALU.add))
                gbp = psR[:, D:D + H * NB].rearrange("p (k b) -> p k b", k=H)
                for src, up, down in ((psO[:, 0:D], ga, gmag), (gbp, gs, gm)):
                    tab(dve.tensor_scalar(up, src, 0.25, None, ALU.max))
                    tab(dve.tensor_scalar(down, src, -0.25, None, ALU.min))

            def more_tables():
                gbp = psR[:, D:D + H * NB].rearrange("p (k b) -> p k b", k=H)
                tabs_done()
                for src, up, down in ((psO[:, 0:D], ga, gmag), (gbp, gs, gm)):
                    tab(dve.scalar_tensor_tensor(up, src, 0.0, up, ALU.is_ge, ALU.mult))
                    tab(dve.scalar_tensor_tensor(down, src, 0.0, down, ALU.is_lt, ALU.mult))
                tabs_done()
                tab(dve.tensor_tensor(ga, ga, gmag, ALU.add))
                tab(dve.tensor_tensor(gbT[:, :, :], gs, gm, ALU.add))
                tabs_done()
                dve.wait_ge(q_affine, 16 * 2)
                tab(dve.tensor_tensor(gag[:, :], ga, gamma_b, ALU.mult))
                tab(dve.tensor_tensor(gab[:, :], ga, beta_b, ALU.mult))
                tabs_done()

            def initial():
                dve.wait_ge(q_bias, 16 * 5)
                tab(dve.tensor_copy(c0hi[:, :], c0[:, :]))
                tabs_done()
                dve.tensor_tensor(c0lo[:, :], c0[:, :], c0hi[:, :].bitcast(f32), ALU.subtract).then_inc(q_tables, 1)

            def adds(sem_in, sem_out, v, tt, back, p, apart):
                if not apart:
                    dve.wait_ge(sem_in, v.lin(4, -4 * back + 2 * tt + H))
                    xb = row(p).rearrange("p (m t n) -> p m t n", m=H, t=2)[:, :, tt, :]
                    dve.tensor_tensor(pre[:, :].rearrange("p (m n) -> p m n", m=H),
                                      psR[:, 0:D].rearrange("p (m n) -> p m n", m=H), xb, ALU.add).then_inc(sem_out, H)
                    return
                for m in range(H):
                    dve.wait_ge(sem_in, v.lin(4, -4 * back + 2 * tt + m + 1))
                    xb = row(p, m * 2 * P + tt * P, P)
                    dve.tensor_tensor(pre[:, m * P:(m + 1) * P], (psR, psF)[m][:, 0:P], xb, ALU.add).then_inc(sem_out, 1)

            def unit1(v, ref):
                rec, norm = has(ref, R1LAG, RP1), has(ref, 1, PAIRS)
                src, dst = xin[:, (ref - 1) % 2, :], htok[:, (ref - 1) % 2, :]

                def count(tt):
                    if has(ref, 1, PAIRS - 1):
                        if tt == 0:
                            dve.wait_ge(a_x[ref % 2], v.half(16, 0, 16))
                            dve.wait_ge(a_mv, v.lin(2))
                            apart(dve)
                        dve.bn_stats(st[:, tt, :], halfw(xin[:, ref % 2, :], tt)).then_inc(a_stats, 1)

                if rec:
                    dve.wait_ge(a_xb, v.lin(1, 1 - R1LAG))
                    adds(a_r, a_pre, v, 0, R1LAG, v.lin(1, SP0 - R1LAG), True)
                if norm:
                    dve.wait_ge(a_stats, v.lin(2))
                    if ref >= 2:
                        dve.wait_ge(a_ve, v.lin(1, -1))
                    apart(dve)
                    for tt in range(2):
                        dve.bn_aggr(mv[:, tt, :], st[:, tt, :]).then_inc(a_mv, 1)
                    if ref == 3:
                        tables()
                    if ref >= 3:
                        dve.wait_ge(a_T, v.lin(1, -2))
                        dve.wait_ge(a_park[(ref - 1) % 2], v.half(16, 1))
                    for tt in range(2):
                        dve.wait_ge(a_mv, v.lin(2, tt - 1))
                        dve.scalar_tensor_tensor(halfw(dst, tt), halfw(src, tt), mv[:, tt, 0:1], ca1,
                                                 ALU.subtract, ALU.mult).then_inc(a_tmp, 1)
                if rec:
                    adds(a_r, a_pre, v, 1, R1LAG, v.lin(1, SP0 - R1LAG), True)
                if has(ref, 3, PAIRS):
                    dve.wait_ge(a_hT, v.lin(1, -2))
                    b = (ref - 3) % 2
                    dve.tensor_tensor(hmT_lo[:, b, :], (psT, psC)[b][:, :], hmT_hi[:, b, :].bitcast(f32),
                                      ALU.subtract).then_inc(a_hl, 1)
                count(0)
                count(1)
                if ref == 4:
                    more_tables()

            def unit2(v, ref):
                rec, post, outp = has(ref, 0, PAIRS), has(ref, 1, PAIRS), has(ref, O0, PAIRS)
                bk = (ref - 1) % 2
                if rec and ref >= G0:
                    adds(s_r, s_pre, v, 0, 0, v.lin(1), False)
                if has(ref, G0 + 1, PAIRS):
                    dve.wait_ge(s_fc, v.lin(1, -G0))
                    dve.wait_ge(s_ig, v.lin(1, -G0))
                    dve.tensor_tensor(cst[:, :, :], gf[:, :, :], gi[:, :, :], ALU.add).then_inc(s_c, 1)
                if post:
                    dve.wait_ge(s_C, v.lin(1))
                    dve.wait_ge(s_h[bk], v.half(16, 1, 16))
                    dve.tensor_tensor(y, psC[:, :], htok[:, bk, :], ALU.add).then_inc(s_y, 1)
                if has(ref, G0 + 1, PAIRS) and pos(ref - 1) < GROUP - 1:
                    dve.wait_ge(s_c, v.lin(1, -G0))
                    dve.wait_ge(s_chi, v.lin(1, -G0 - grp(ref - 1)))
                    dve.tensor_tensor(clo[:, :, :], cst[:, :, :], chi[:, :, :].bitcast(f32), ALU.subtract).then_inc(s_clo, 1)
                if has(ref, 2, PAIRS):
                    dve.wait_ge(s_stB, v.lin(2, -2))
                    if ref >= 3:
                        dve.wait_ge(s_veB, v.lin(1, -2))
                    apart(dve)
                    for tt in range(2):
                        dve.bn_aggr(mvb[:, tt, :], stb[:, tt, :]).then_inc(s_mvB, 1)
                if post:
                    dve.wait_ge(s_y, v.lin(1))
                    apart(dve)
                    for tt in range(2):
                        dve.bn_stats(st[:, tt, :], halfw(y, tt)).then_inc(s_stA, 1)
                if has(ref, 2, PAIRS):
                    if ref >= 3:
                        dve.wait_ge(s_T, v.lin(1, -2))
                    for tt in range(2):
                        dve.wait_ge(s_mvB, v.lin(2, tt - 3))
                        dve.scalar_tensor_tensor(halfw(h2tok, tt), row(v.lin(1, -2), tt * D, D), mvb[:, tt, 0:1],
                                                 cb1[:, :], ALU.subtract, ALU.mult).then_inc(s_tmpB, 1)
                if post:
                    dve.wait_ge(s_stA, v.lin(2))
                    apart(dve)
                    for tt in range(2):
                        dve.bn_aggr(mv[:, tt, :], st[:, tt, :]).then_inc(s_mvA, 1)
                    dve.wait_ge(s_mvA, v.lin(2))
                    for tt in range(2):
                        dve.scalar_tensor_tensor(halfw(y, tt), halfw(y, tt), mv[:, tt, 0:1], gag[:, :],
                                                 ALU.subtract, ALU.mult).then_inc(s_tmpA, 1)
                if rec:
                    if ref >= G0:
                        adds(s_r, s_pre, v, 1, 0, v.lin(1), False)
                    if ref == SP0 - 1:
                        dve.wait_ge(s_tanh, 4 * SP0)
                        dve.tensor_copy(h_skip[:, :].rearrange("p (m n) -> p m n", m=H), hs[:, 1, :, :]).then_inc(s_skip, 1)
                if has(ref, 3, PAIRS):
                    for m in range(H):
                        dve.wait_ge(s_hi, v.lin(2, -6 + H))
                        dve.tensor_tensor(ring(lo, v, ref, 3, m), tposed(m), ring(hi, v, ref, 3, m).bitcast(f32),
                                          ALU.subtract).then_inc(s_lo, 1)
                if post:
                    dve.wait_ge(s_rA, v.lin(1))
                    dve.wait_ge(s_xg, v.lin(1))
                    for tt in range(2):
                        dve.wait_ge(s_tmpA, v.lin(2, -1 + tt))
                        dve.scalar_tensor_tensor(row(v.lin(1, -1), tt * D, D), halfw(y, tt), rstd[:, tt:tt + 1],
                                                 halfw(xin[:, bk, :], tt), ALU.mult, ALU.add).then_inc(s_x1, 1)
                if post:
                    for tt in range(2):
                        dve.wait_ge(s_x1, v.lin(2, tt - 1))
                        apart(dve)
                        dve.bn_stats(stb[:, tt, :], row(v.lin(1, -1), tt * D, D)).then_inc(s_stB, 1)
                if outp:
                    dve.wait_ge(s_W, v.lin(1, -O0 + 1))
                    if pos(ref) == 0:
                        dve.wait_ge(s_u, 2 * ((ref - O0) // GROUP + 1))
                    if ref == TAIL + 1:
                        dve.wait_ge(s_T, PAIRS)
                    elif ref > O0 and ref != TAIL:
                        dve.wait_ge(s_TO, v.lin(1, -O0 if ref < TAIL else -O0 - 2))
                    p = v.lin(1, -O0 - GROUP * ((ref - O0) // GROUP))
                    for m in range(H):
                        dve.tensor_tensor(
                            ow_of(ref)[:, m * GC:(m + 1) * GC].rearrange("p (t b k) -> p b t k", t=2, b=NB),
                            psW_of(ref)[:, m * GC:(m + 1) * GC].rearrange("p (b t k) -> p b t k", b=NB, t=2),
                            uvec[:, m:m + 1, bass.ds(p * (2 * K), 2 * K)].rearrange("p o (t k) -> p o t k", t=2)
                            .broadcast_to([P, NB, 2, K]),
                            ALU.add).then_inc(s_ws, 1)
                back = back_of(ref)
                if back:
                    dve.wait_ge(s_TO, v.lin(1, 1 - O0 - back))
                    x1 = row(v.lin(1, -O0 - back))
                    dve.tensor_tensor(x1, psO_of(ref - back)[:, :], x1, ALU.add).then_inc(s_fin, 1)
                if has(ref, G0, PAIRS):
                    dve.wait_ge(s_f, v.lin(2, -2 * G0 + 2))
                    if pos(ref) == 0:
                        prev = c0[:, :].rearrange("p (m o) -> p m o", o=1).broadcast_to([P, H, GC])
                    else:
                        prev = cst[:, :, :]
                    dve.tensor_tensor(gf[:, :, :], gf[:, :, :], prev, ALU.mult).then_inc(s_fc, 1)
                if ref == 1:
                    initial()
                if ref == G0 - 2:
                    dve.wait_ge(q_uc0, 1)
                    uc0 = psW[:, 0:3 * H * C0W].rearrange("p (n m c) -> p n m c", n=3, m=H)[:, :, :, 0]
                    dve.tensor_tensor(bias0[:, :, :], uc0, bias[:, 0:3, :], ALU.add).then_inc(q_bias0, 1)
                if ref == PAIRS + 1:
                    dve.tensor_tensor(pre[:, :].rearrange("p (m n) -> p m n", m=H), hs[:, 1, :, :],
                                      h_end[:, :].rearrange("p (m n) -> p m n", m=H), ALU.subtract).then_inc(k_diff, 1)
                    dve.wait_ge(k_diff, 1)
                    near = y[:, 0:D]
                    dve.tensor_scalar(near, pre[:, :], -TOL, None, ALU.is_ge).then_inc(k_diff, 1)
                    dve.wait_ge(k_diff, 2)
                    dve.scalar_tensor_tensor(pre[:, :], pre[:, :], TOL, near, ALU.is_le, ALU.mult).then_inc(k_diff, 1)
                    dve.wait_ge(k_diff, 3)
                    dve.reduce_sum(cnt[:, :], pre[:, :], AX.X).then_inc(k_diff, 1)
                if ref == TAIL - 1:
                    dve.wait_ge(k_sum, 1)
                    dve.tensor_scalar(miss[:, :], psR[0:1, 0:1], P * D - 0.5, float(K), ALU.is_lt, ALU.mult).then_inc(k_diff, 1)
                    dve.wait_ge(k_diff, 5)
                    dve.tensor_copy(again[:, :], miss[:, :]).then_inc(k_flag, 1)

            def body():
                n_tab[0] = 0
                prepare()
                dve.tensor_copy(hs[:, 1, :, :], h_skip[:, :].rearrange("p (m n) -> p m n", m=H)).then_inc(a_end, 1)
                walk(dve, RUNS1, unit1)
                dve.wait_ge(a_tanh, 4 * RP1)
                dve.tensor_copy(h_end[:, :].rearrange("p (m n) -> p m n", m=H), hs[:, 1, :, :]).then_inc(a_end, 1)
                dve.wait_ge(a_end, 2)
                to = hs[:, 1, :, :].rearrange("p m (b k) -> p (m b) k", b=NB)
                dve.tensor_copy(to[:, :, 1:K], h_end[:, :].rearrange("p (m k) -> p m k", k=K)[:, :, 0:K - 1]).then_inc(a_end, 1)
                dve.memset(to[:, :, 0:1], 0.0).then_inc(a_end, 1)
                dve.wait_ge(a_xb, PAIRS)
                walk(dve, RUNS2, unit2)

            rounds(dve, body, "dve")

        @block.tensor
        def _(pe):
            pe.wait_ge(q_ident, 6)

            def table(j, ps):
                pe.wait_ge(q_wm[j], 16)
                for k in range(H):
                    last = pe.matmul(ps[:, :], scE[:, k, :, :].rearrange("p b n -> p (b n)"), wm[j][:, k, :],
                                     start=(k == 0), stop=(k == H - 1))
                last.then_inc(q_mod, 1)

            def weight(name):
                pe.wait_ge(q_w[name], 16)
                last, split = place(name)
                if last is None and BANK[name] is psO:
                    pe.wait_ge(q_tab, 14)
                if last is not None:
                    pe.wait_ge(q_whi, last + 1)
                    if split:
                        pe.wait_ge(q_wcopy, split)
                for k in range(H):
                    for m in range(H):
                        ins = pe.transpose(BANK[name][:, k * D + m * P:k * D + (m + 1) * P],
                                           raw[name][:, m, k * P:(k + 1) * P], ident[:, :])
                ins.then_inc(q_wT, 1)

            def prepare():
                pe.wait_ge(q_silu, 1)
                for k in range(H):
                    last = pe.transpose(psR[:, k * NB:(k + 1) * NB], csig[:, k * P:(k + 1) * P], ident[0:NB, 0:NB])
                last.then_inc(q_scTp, 1)
                pe.wait_ge(q_scT, 2)
                table(0, psC)
                weight("B")
                weight("A")

            def tables():
                table(1, psO)
                table(2, psF)
                for m in range(H):
                    for k in range(H):
                        last = pe.matmul(psR[:, D + m * NB:D + (m + 1) * NB], wm[2][:, k, D + m * P:D + (m + 1) * P],
                                         scT[:, k, :], start=(k == 0), stop=(k == H - 1))
                last.then_inc(q_mod, 1)

            def recur(sem_in, sem_free, sem_out, v, tt, back, first, apart, xb=None):
                for k in range(H):
                    if not first:
                        pe.wait_ge(sem_in, v.lin(4, -4 * back + 2 * tt - 1 + k))
                    for m in range(H):
                        if k == 0 and m == 1 and apart and not first:
                            pe.wait_ge(sem_free, v.lin(4, -4 * back + 2 * tt))
                        ps = (psR, psF)[m][:, 0:P] if apart else psR[:, m * P:(m + 1) * P]
                        ins = pe.matmul(ps, AT[:, k, m * P:(m + 1) * P], hs[:, 1 - tt, k, :],
                                        start=(k == 0 and (apart or m == 0)),
                                        stop=(k == H - 1 and (apart or m == H - 1) and xb is None), skip_group_check=True)
                        if k == H - 1 and xb is not None:
                            ins = pe.matmul(ps, ident[:, :], xb(m), start=False, stop=True, skip_group_check=True)
                        if k == H - 1 and apart:
                            ins.then_inc(sem_out, 1)
                if not apart:
                    ins.then_inc(sem_out, H)

            def unit1(v, ref):
                rec = has(ref, R1LAG, RP1)
                if rec:
                    if ref == R1LAG:
                        pe.wait_ge(q_tab, 14)
                        pe.wait_ge(a_end, 1)
                        pe.wait_ge(q_whi, 2)
                    recur(a_tanh, a_pre, a_r, v, 0, R1LAG, ref == R1LAG, True)

                def times_b(back, first, end):
                    if not has(ref, back, PAIRS):
                        return
                    if first == 0:
                        if ref == back:
                            pe.wait_ge(q_whi, 1)
                            pe.wait_ge(q_wlo, 1)
                        elif ref == back + 1:
                            pe.wait_ge(q_tab, 14)
                        else:
                            pe.wait_ge(a_xb, v.lin(1, -1 - back))
                        pe.wait_ge(a_hT, v.lin(1, 1 - back))
                        pe.wait_ge(a_hl, v.lin(1, 1 - back))
                    for n in range(first, end):
                        m, k = n // (3 * H), n // 3 % H
                        w, h = ((whi, hmT_hi), (whi, hmT_lo), (wlo, hmT_hi))[n % 3]
                        ps = (psW, psO)[(ref - back) % 2]
                        last = pe.matmul(ps[:, m * 2 * P:(m + 1) * 2 * P], w["B"][:, k, m * P:(m + 1) * P],
                                         h[:, (ref - back) % 2, k * 2 * P:(k + 1) * 2 * P],
                                         start=(n % (3 * H) == 0), stop=(n % (3 * H) == 3 * H - 1))
                    if end == 3 * H * H:
                        last.then_inc(a_B, 1)

                times_b(4, 0, 8)
                if rec:
                    recur(a_tanh, a_pre, a_r, v, 1, R1LAG, False, True)
                times_b(4, 8, 3 * H * H)
                if has(ref, 2, PAIRS):
                    if ref >= 4:
                        pe.wait_ge(a_hT, v.lin(1, -3))
                        pe.wait_ge(a_hl, v.lin(1, -3))
                    for tt in range(2):
                        pe.wait_ge(a_h, v.lin(2, tt - 3))
                        for m in range(H):
                            last = pe.transpose((psT, psC)[ref % 2][:, m * 2 * P + tt * P:m * 2 * P + (tt + 1) * P],
                                                htok[:, ref % 2, tt * D + m * P:tt * D + (m + 1) * P], ident[:, :])
                    last.then_inc(a_T, 1)
                if ref == 0:
                    tables()
                if ref == 3:
                    weight("C")

            def split3(ps, name, xhi, xlo, start, stop, at=0, columns=GC):
                n = 0
                for m in range(H):
                    for k in range(H):
                        for w, xx in ((whi, xhi), (whi, xlo), (wlo, xhi)):
                            n += 1
                            last = pe.matmul(ps[:, at + m * columns:at + (m + 1) * columns],
                                             w[name][:, k, m * P:(m + 1) * P], xx(k),
                                             start=(start and n == 1), stop=(stop and n == 6 * H), skip_group_check=True)
                return last

            def output(v, ref):
                if not has(ref, O0, PAIRS):
                    return
                if ref in (TAIL, TAIL + 1):
                    pe.wait_ge((s_f, s_g)[ref - TAIL], 2 * PAIRS)
                elif ref > O0:
                    pe.wait_ge(s_ws, v.lin(2, -2 * O0 if ref < TAIL else -2 * O0 - 4))
                og = (ref - O0) // GROUP
                p = v.lin(1, -O0 - GROUP * og)
                split3(psW_of(ref), "wo", lambda k: hi[:, og % 2, k, :, bass.ds(p * (2 * K), 2 * K)],
                       lambda k: lo[:, og % 2, k, :, bass.ds(p * (2 * K), 2 * K)], True, True).then_inc(s_W, 1)

            def unit2(v, ref):
                rec, gates = has(ref, 0, PAIRS), has(ref, G0, PAIRS)
                g, b = grp(ref), v.lin(1, -G0 - GROUP * grp(ref))

                def project(tt, back):
                    if ref - back < CS:
                        pe.wait_ge(s_tanh, v.lin(4, -4 * back + 2 * tt + 2))
                        for k in range(H):
                            last = pe.matmul(psC[:, tt * D:(tt + 1) * D], hs[:, tt, k, :], whole("C")[:, k, :],
                                             start=(k == 0), stop=(k == H - 1))
                        return last
                    pe.wait_ge(s_hsh, v.lin(2, -2 * back - 2 * CS + tt + 1))
                    pe.wait_ge(s_hsl, v.lin(2, -2 * back - 2 * CS + tt + 1))
                    n = 0
                    for k in range(H):
                        for h, c in ((hs_hi, whi), (hs_hi, wlo), (hs_lo, whi)):
                            n += 1
                            last = pe.matmul(psC[:, tt * D:(tt + 1) * D], h[:, tt, k, :], c["C"][:, k, :],
                                             start=(n == 1), stop=(n == 3 * H))
                    return last

                def next_h(tt):
                    if ref < G0:
                        recur(s_tanh, s_tanh, s_r, v, tt, 0, ref == 0 and tt == 0, True,
                              lambda m: row(v.lin(1), m * 2 * P + tt * P, P))
                    else:
                        recur(s_tanh, s_tanh, s_r, v, tt, 0, False, False)

                def gate_x(n):
                    if not gates:
                        return
                    if n == 0 and pos(ref) == 0:
                        pe.wait_ge(s_hi, 2 * GROUP * (g + 1))
                        pe.wait_ge(s_lo, 2 * GROUP * (g + 1))
                    if ref > G0:
                        pe.wait_ge((s_f, s_i, s_g)[n], v.lin(2, -2 * G0))
                    last = split3(
                           (psF, psI, psG)[n], ("wf", "wi", "wc")[n],
                           lambda k: hi[:, g % 2, k, bass.ds(b, 1), :].rearrange("p o n -> p (o n)"),
                           lambda k: lo[:, g % 2, k, bass.ds(b, 1), :].rearrange("p o n -> p (o n)"), True, pos(ref) == 0)
                    if pos(ref) == 0:
                        last.then_inc(s_gate, 1)

                def gate_c(n):
                    if not gates or pos(ref) == 0:
                        return
                    if n == 0:
                        pe.wait_ge(s_chi, v.lin(1, -G0 - g))
                        pe.wait_ge(s_clo, v.lin(1, -G0 - g))
                    split3((psF, psI, psG)[n], ("uf", "ui", "uc")[n], lambda k: chi[:, k, :], lambda k: clo[:, k, :],
                           False, True).then_inc(s_gate, 1)

                if ref == G0 - 2:
                    pe.wait_ge(q_whi, len(NAMES))
                    pe.wait_ge(q_wlo, len(whi))
                    pe.wait_ge(q_tables, 1)
                    for n, name in enumerate(("uf", "ui", "uc")):
                        last = split3(psW, name, lambda k: c0hi[:, k:k + 1].broadcast_to([P, C0W]),
                                      lambda k: c0lo[:, k:k + 1].broadcast_to([P, C0W]), n == 0, n == 2, n * H * C0W, C0W)
                    last.then_inc(q_uc0, 1)
                if rec:
                    if ref == 0:
                        pe.wait_ge(a_end, 4)
                    next_h(0)
                if has(ref, 1, PAIRS):
                    project(1, 1).then_inc(s_C, 1)
                if ref <= TAIL:
                    output(v, ref)
                back = back_of(ref)
                if back:
                    pe.wait_ge(s_ob, v.lin(2, 2 - 2 * O0 - 2 * back))
                    if ref - back == TAIL:
                        pe.wait_ge(s_i, 2 * PAIRS)
                    elif ref - back > O0:
                        pe.wait_ge(s_fin, v.lin(1, -O0 - back if ref - back < TAIL else -O0 - back - 1))
                    for tt in range(2):
                        for m in range(H):
                            last = pe.transpose(psO_of(ref - back)[:, tt * D + m * P:tt * D + (m + 1) * P],
                                                ow_of(ref - back)[:, m * GC + tt * P:m * GC + (tt + 1) * P], ident[:, :])
                    last.then_inc(s_TO, 1)
                gate_x(0)
                if has(ref, 3, PAIRS):
                    pe.wait_ge(s_h2, v.lin(1, -2))
                    if ref > 3:
                        pe.wait_ge(s_hi, v.lin(2, -6))
                        pe.wait_ge(s_lo, v.lin(2, -6))
                    for tt in range(2):
                        for m in range(H):
                            last = pe.transpose(psT[:, m * 2 * P + tt * P:m * 2 * P + (tt + 1) * P],
                                                h2tok[:, tt * D + m * P:tt * D + (m + 1) * P], ident[:, :])
                    last.then_inc(s_T, 1)
                if rec:
                    next_h(1)
                if ref == PAIRS + 2:
                    pe.wait_ge(k_diff, 4)
                    pe.matmul(psR[0:1, 0:1], cnt[:, :], ones[:, :], start=True, stop=True).then_inc(k_sum, 1)
                if ref == TAIL:
                    output(At(0, TAIL + 1), TAIL + 1)
                if has(ref, O0, PAIRS) and pos(ref) == 0:
                    pe.wait_ge(s_c, ref - G0)
                    pe.wait_ge(s_y, min(ref, PAIRS))
                    for m in range(H):
                        for k in range(H):
                            last = pe.matmul(psC[:, m * GC:(m + 1) * GC], uoT[:, k, m * P:(m + 1) * P], cst[:, k, :],
                                             start=(k == 0), stop=(k == H - 1))
                    last.then_inc(s_U, 1)
                if ref >= TAIL:
                    output(At(0, ref + 2), ref + 2)
                gate_x(1)
                gate_x(2)
                if rec:
                    if ref >= 1:
                        pe.wait_ge(s_y, v.lin(1))
                    if has(ref, O0, PAIRS) and pos(ref) == 0:
                        pe.wait_ge(s_u, 2 * ((ref - O0) // GROUP + 1))
                    project(0, 0)
                if ref < len(LATE):
                    weight(LATE[ref])
                gate_c(0)
                gate_c(1)
                gate_c(2)

            def body():
                prepare()
                walk(pe, RUNS1, unit1)
                pe.wait_ge(q_whi, len(EARLY))
                pe.wait_ge(q_wlo, 2)
                walk(pe, RUNS2, unit2)

            rounds(pe, body, "pe")


_INS = ["L0_attn_x", "L0_attn_A", "L0_attn_B", "L0_attn_C", "L0_attn_gamma", "L0_attn_beta",
        "L0_ffn_wf", "L0_ffn_uf", "L0_ffn_bf", "L0_ffn_wi", "L0_ffn_ui", "L0_ffn_bi", "L0_ffn_wc", "L0_ffn_uc",
        "L0_ffn_bc", "L0_ffn_wo", "L0_ffn_uo", "L0_ffn_bo", "L0_ffn_in_c", "L0_c", "L0_wmod"]


def kernel(**inputs):
    import numpy as _np
    import concourse.bacc as _bacc
    from concourse import mybir as _mybir
    from concourse.bass_utils import run_bass_kernel_spmd as _run

    nc = _bacc.Bacc("TRN2", target_bir_lowering=False, num_devices=1)
    arrays, args = {}, []
    for name in _INS:
        a = _np.ascontiguousarray(inputs[name])
        arrays[f"in_{name}_dram"] = a
        args.append(nc.dram_tensor(f"in_{name}_dram", a.shape, _mybir.dt.from_np(a.dtype), kind="ExternalInput").ap())
    shape = inputs["L0_attn_x"].shape
    args.append(nc.dram_tensor("out_0_dram", shape, _mybir.dt.float32, kind="ExternalOutput").ap())
    adaln_kernel(nc, *args)
    r = _run(nc, [arrays], core_ids=[0])
    return r.results[0]["out_0_dram"]
```
